# Optimizing a Trainium2 kernel written in Bass

```python
import numpy as np
import jax
import jax.numpy as jnp

def _softmax(x, axis=-1):
    return jax.nn.softmax(x, axis=axis)

def _gelu(x):
    return jax.nn.gelu(x, approximate=True)

def _silu(x):
    return jax.nn.silu(x)

def _sigmoid(x):
    return jax.nn.sigmoid(x)

def _layernorm(x, axis=-1, eps=1e-05):
    m = jnp.mean(x, axis=axis, keepdims=True)
    v = jnp.var(x, axis=axis, keepdims=True)
    return (x - m) / jnp.sqrt(v + eps)

def _scatter_add(tgt, idx, src, axis=0):
    return tgt.at[idx].add(src)

def _segment_sum(src, seg, n):
    return jax.ops.segment_sum(src, seg, n)
kernel_name = 'mk_gnn_ffn_d1_gnn_r16_bab052'

def setup_inputs(seed: int=0):
    np.random.seed(seed)
    _w = jnp.asarray

    def _rec_inputs():
        import jax
        import jax.numpy as jnp
        _gk = jax.random.key(seed)
        x = -0.0002117 + 1 * jax.random.normal(jax.random.fold_in(_gk, 1), (6250, 256), jnp.float32)
        src = jax.random.randint(jax.random.fold_in(_gk, 2), (100000,), 0, 6250, jnp.int32)
        dst = jax.random.randint(jax.random.fold_in(_gk, 3), (100000,), 0, 6250, jnp.int32)
        _o = jnp.argsort(dst, stable=True)
        src = src[_o]
        dst = dst[_o]
        edge_weight = jax.random.uniform(jax.random.fold_in(_gk, 12), (100000,), jnp.float32, 0.0, 1)
        return (x, src, dst, edge_weight)
    x, src, dst, edge_weight = _rec_inputs()

    def _L0_gnn_setup():
        import jax, jax.numpy as jnp
        import numpy as np
        N_NODES = 6250
        N_EDGES = 200000
        D_IN = 256
        D_OUT = 256
        key = jax.random.key(seed)
        k1, k2, k3, k4, k5 = jax.random.split(key, 5)
        x = jax.random.normal(k1, (N_NODES, D_IN), dtype=jnp.float32)
        W = jax.random.normal(k2, (D_OUT, D_IN), dtype=jnp.float32) * (1.0 / np.sqrt(D_IN))
        edge_row = jax.random.randint(k3, (N_EDGES,), 0, N_NODES, dtype=jnp.int32)
        edge_col = jax.random.randint(k4, (N_EDGES,), 0, N_NODES, dtype=jnp.int32)
        edge_val = jax.random.uniform(k5, (N_EDGES,), dtype=jnp.float32)
        return {'x': x, 'W': W, 'edge_row': edge_row, 'edge_col': edge_col, 'edge_val': edge_val}
    _L0_gnn_all = _L0_gnn_setup()
    _L0_gnn_in = {k: v for k, v in _L0_gnn_all.items() if k in ('W',)}
    del _L0_gnn_all

    def _L0_ffn_setup():
        import jax, jax.numpy as jnp
        import numpy as np
        B, S, H, F, E, K = (8, 256, 256, 512, 16, 2)
        EPS = 1e-05
        key = jax.random.key(seed)
        ks = jax.random.split(key, 9)
        sc = 0.02
        return {'x': jax.random.normal(ks[0], (B, S, H), dtype=jnp.float32), 'gate_w': jax.random.normal(ks[1], (H, E), dtype=jnp.float32) * sc, 'gate_b': jnp.zeros((E,), dtype=jnp.float32), 'w1': jax.random.normal(ks[2], (E, H, F), dtype=jnp.float32) * sc, 'b1': jnp.zeros((E, F), dtype=jnp.float32), 'w2': jax.random.normal(ks[3], (E, F, H), dtype=jnp.float32) * sc, 'b2': jnp.zeros((E, H), dtype=jnp.float32), 'gamma': jnp.ones((H,), dtype=jnp.float32), 'beta': jnp.zeros((H,), dtype=jnp.float32)}
    _L0_ffn_all = _L0_ffn_setup()
    _L0_ffn_in = {k: v for k, v in _L0_ffn_all.items() if k in ('gate_w', 'gate_b', 'w1', 'b1', 'w2', 'b2', 'gamma', 'beta')}
    del _L0_ffn_all
    return {'x': x, 'src': src, 'dst': dst, 'edge_weight': edge_weight, 'L0_gnn_W': _L0_gnn_in['W'], 'L0_ffn_gate_w': _L0_ffn_in['gate_w'], 'L0_ffn_gate_b': _L0_ffn_in['gate_b'], 'L0_ffn_w1': _L0_ffn_in['w1'], 'L0_ffn_b1': _L0_ffn_in['b1'], 'L0_ffn_w2': _L0_ffn_in['w2'], 'L0_ffn_b2': _L0_ffn_in['b2'], 'L0_ffn_gamma': _L0_ffn_in['gamma'], 'L0_ffn_beta': _L0_ffn_in['beta']}

def reference(x, src, dst, edge_weight, L0_gnn_W, L0_ffn_gate_w, L0_ffn_gate_b, L0_ffn_w1, L0_ffn_b1, L0_ffn_w2, L0_ffn_b2, L0_ffn_gamma, L0_ffn_beta):
    import jax
    import jax.numpy as jnp

    def _L0_gnn_ref(x, W, edge_row, edge_col, edge_val):
        import jax, jax.numpy as jnp
        import numpy as np
        N_NODES = 6250
        N_EDGES = 200000
        D_IN = 256
        D_OUT = 256
        h = jnp.einsum('nd,od->no', x, W)
        msgs = edge_val[:, None] * h[edge_col]
        out = jax.ops.segment_sum(msgs, edge_row, num_segments=N_NODES)
        return out

    def _L0_ffn_ref(x, gate_w, gate_b, w1, b1, w2, b2, gamma, beta):
        import jax, jax.numpy as jnp
        import numpy as np
        B, S, H, F, E, K = (8, 256, 256, 512, 16, 2)
        EPS = 1e-05
        gate_logits = x @ gate_w + gate_b
        topk_vals, topk_idx = jax.lax.top_k(gate_logits, K)
        topk_w = jax.nn.softmax(topk_vals, axis=-1)
        h = jax.nn.relu(jnp.einsum('bsh,ehf->bsef', x, w1) + b1)
        expert_out = jnp.einsum('bsef,efh->bseh', h, w2) + b2
        sel = jnp.take_along_axis(expert_out, topk_idx[:, :, :, None], axis=2)
        moe = jnp.sum(topk_w[..., None] * sel, axis=2)
        y = x + moe
        mu = jnp.mean(y, axis=-1, keepdims=True)
        var = jnp.var(y, axis=-1, keepdims=True)
        return (y - mu) / jnp.sqrt(var + EPS) * gamma + beta
    x = x + _L0_gnn_ref(_layernorm(x, axis=-1), L0_gnn_W, src, dst, edge_weight)
    x = x + _L0_ffn_ref(_layernorm(x, axis=-1)[None], L0_ffn_gate_w, L0_ffn_gate_b, L0_ffn_w1, L0_ffn_b1, L0_ffn_w2, L0_ffn_b2, L0_ffn_gamma, L0_ffn_beta)[0]
    return x

_drawn_inputs = setup_inputs


def setup_inputs(seed=0):
    import zlib

    import numpy as np

    out = dict(_drawn_inputs(seed))
    spreads = {'L0_ffn_gate_b': (0.0, 0.403),
     'L0_ffn_b1': (0.0, 0.8),
     'L0_ffn_b2': (0.0, 0.386),
     'L0_ffn_gamma': (1.0, 0.2),
     'L0_ffn_beta': (0.0, 0.287)}
    factors = {'L0_ffn_w1': 3.244}
    for name, (base, spread) in spreads.items():
        noise = np.random.default_rng([zlib.crc32(name.encode()), seed]).standard_normal(out[name].shape)
        drawn = base * np.exp(spread * noise) if base else spread * noise
        out[name] = jnp.asarray(drawn.astype(out[name].dtype))
    for name, factor in factors.items():
        out[name] = (out[name] * factor).astype(out[name].dtype)
    return out
```

```python
import concourse.bass as bass
from concourse import mybir
from contextlib import ExitStack


class Chain:

    def __init__(self, engine, done):
        self.engine, self.done, self.base, self.n, self.per, self.turn = engine, done, 0, 0, 0, 0

    def enter(self, turn, per):
        if not self.per:
            self.base += self.n
        self.turn, self.per, self.n = turn, per, 0

    def leave(self, turns):
        assert self.n == self.per, (self.n, self.per)
        self.base, self.per, self.turn, self.n = self.base + turns * self.per, 0, 0, 0

    def __call__(self, instruction):
        instruction.then_inc(self.done, 1)
        self.n += 1
        self.engine.wait_ge(self.done, self.turn * self.per + (self.base + self.n))


def await_turn(engine, sem, turn, per, value):
    if isinstance(turn, int):
        if per * turn + value > 0:
            engine.wait_ge(sem, per * turn + value)
    else:
        engine.wait_ge(sem, turn * per + value)


def gnn_moe_kernel(nc, x, src, dst, edge_weight, gnn_w, gate_w, gate_b, w1, b1, w2, b2, gamma, beta, out):
    fp32, bf16, i32, u32 = mybir.dt.float32, mybir.dt.bfloat16, mybir.dt.int32, mybir.dt.uint32
    ALU, ACT, AX = mybir.AluOpType, mybir.ActivationFunctionType, mybir.AxisListType
    ds = bass.ds

    P = 128
    N, D = x.shape
    NE = src.shape[0]
    EX, _, F = w1.shape
    EPS = 1e-5
    NB = D // P
    NW = -(-N // P)
    WB = 7
    WT = NW // WB
    assert WB * WT == NW
    NP = NW * P
    LASTW = N - (NW - 1) * P
    GT = 8
    GE = GT * P
    NG = -(-NE // GE)
    NG += NG % 2
    FULL = NE // GE
    REST = NE - FULL * GE
    COPIES = 4
    JUNK = NP
    ROWS = NP + P
    GB = 2
    GTURNS = NG // GB
    PAIRS = GT // 2
    PT = GB * PAIRS

    FB = F // P
    CAP = NP + P
    RW = 320
    TOKEN, CHOICE = D, D + 1
    slots_dram = nc.dram_tensor("slots", [EX * CAP, RW], fp32).ap()
    y_dram = nc.dram_tensor("expert_out", [2 * NP + P, D], fp32).ap()
    h_rows_dram = nc.dram_tensor("h_rows", [NP, D], fp32).ap()
    src_dram = nc.dram_tensor("src_padded", [NG, GE], i32).ap()
    table_dram = nc.dram_tensor("group_table", [NG, 2], fp32).ap()
    acc = [nc.dram_tensor(f"acc{c}", [ROWS, D], fp32).ap() for c in range(COPIES)]

    ctx = ExitStack()
    with ctx:
        def sb(name, shape, dt):
            return ctx.enter_context(nc.sbuf_tensor(name, shape, dt))

        def bank(name, shape, dt=fp32):
            return ctx.enter_context(nc.psum_tensor(name, shape, dt))

        def sem(name):
            return ctx.enter_context(nc.semaphore(name))

        zeros = sb("zeros", [P, 10 * D], fp32)
        ones = sb("ones", [P, P], fp32)
        ident = sb("ident", [P, P], fp32)
        iota_i = sb("iota_i", [P, P], i32)
        iota_f = sb("iota_f", [P, P], fp32)
        part_i = sb("part_i", [P, 1], i32)
        part_f = sb("part_f", [P, 1], fp32)
        junk_row = sb("junk_row", [P, 1], fp32)
        before = sb("before", [P, P], fp32)
        eps = sb("eps", [P, 1], fp32)

        x1 = sb("x1", [P, NW, D], fp32)
        rstd2 = sb("rstd2", [P, NW], fp32)
        shift2 = sb("shift2", [P, NW], fp32)
        top2 = sb("top2", [P, NW, 2], fp32)
        first_w = sb("first_w", [P, NW], fp32)
        second_w = sb("second_w", [P, NW], fp32)
        upper = sb("upper", [P, P], bf16)
        ones_b = sb("ones_b", [P, P], bf16)
        gate_sb = sb("gate_sb", [P, NB, EX], fp32)
        gate_bb = sb("gate_bb", [P, EX], fp32)
        expert_base = sb("expert_base", [P, EX], fp32)
        carry = sb("carry", [P, EX], bf16)
        carry_f = sb("carry_f", [P, EX], fp32)
        filler = sb("filler", [P, RW], fp32)
        tok = sb("tok", [P, WB], fp32)
        counts_f = sb("counts_f", [1, EX], fp32)
        counts_i = sb("counts_i", [1, EX], i32)
        ntiles_i = sb("ntiles_i", [1, EX], i32)
        ntiles_f = sb("ntiles_f", [1, EX], fp32)
        ends_f = sb("ends_f", [1, EX], fp32)
        tiles_i = sb("tiles_i", [1, EX + 1], i32)
        w1_sb = sb("w1_sb", [P, 2, NB, F], fp32)
        w2_sb = sb("w2_sb", [P, 2, FB, D], fp32)
        b1_rows = sb("b1_rows", [EX * FB, P], fp32)
        b1_cols = sb("b1_cols", [P, EX * FB], fp32)
        b2_b = sb("b2_b", [P, EX, D], fp32)
        gamma_b = sb("gamma_b", [P, D], fp32)
        beta_b = sb("beta_b", [P, D], fp32)

        layer1 = ctx.enter_context(ExitStack())

        def sb(name, shape, dt):
            return layer1.enter_context(nc.sbuf_tensor(name, shape, dt))

        table_b = sb("table_b", [P, NG, 2], fp32)
        table_i = sb("table_i", [1, NG * 2], i32)
        gathers_i = sb("gathers_i", [1, NG], i32)
        SRC, WGT, REL, OFF, DST = range(5)
        cols = sb("cols", [P, NG, 5, GT], fp32)

        prepare = ctx.enter_context(ExitStack())

        def sb(name, shape, dt):
            return prepare.enter_context(nc.sbuf_tensor(name, shape, dt))

        stats = sb("stats", [P, NW, 6], fp32)
        mv = sb("mv", [P, NW, 2], fp32)
        upper_f = sb("upper_f", [P, P], fp32)
        std = sb("std", [P, NW], fp32)
        rstd = sb("rstd", [P, NW], fp32)
        shift = sb("shift", [P, NW], fp32)
        xn = sb("xn", [P, WB, D], fp32)
        xnT = sb("xnT", [P, 2, NB, P], fp32)
        w_rows = sb("w_rows", [P, NB, D], fp32)
        wT = sb("wT", [P, NB, D], fp32)
        h_stage = sb("h_stage", [P, WB, D], fp32)
        src_rows = sb("src_rows", [NG, GE], i32)
        dst_rows = sb("dst_rows", [NG, GE], i32)
        wgt_rows = sb("wgt_rows", [NG, GE], fp32)
        src_rf = sb("src_rf", [NG, GE], fp32)
        dst_rf = sb("dst_rf", [NG, GE], fp32)
        lohi = sb("lohi", [NG, 2], fp32)
        span = sb("span", [NG, 1], fp32)
        table = sb("table", [NG, 2], fp32)
        slow_f = sb("slow_f", [1, NG], fp32)
        slows_f = sb("slows_f", [1, NG], fp32)

        bk = [bank(f"bank{i}", [P, 512]) for i in range(8)]

        x_in = [sem(f"x_in{t}") for t in range(WT)]
        w_in = sem("w_in")
        pads_set = sem("pads_set")
        edges_in = sem("edges_in")
        consts = sem("consts")
        zero_set = sem("zero_set")
        acc_init = sem("acc_init")
        pool_own = sem("pool_own")
        dve_own = sem("dve_own")
        dve_step = sem("dve_step")
        pool_steps = sem("pool_steps")
        dve_steps = sem("dve_steps")
        pe_steps = sem("pe_steps")
        sp_steps = sem("sp_steps")
        later_in = sem("later_in")
        b1_in = sem("b1_in")
        b1_turned = sem("b1_turned")
        w_t = sem("w_t")
        wT_ready = sem("wT_ready")
        mv_ready = sem("mv_ready")
        std_ready = sem("std_ready")
        shift_ready = sem("shift_ready")
        xn_ready = sem("xn_ready")
        xn_turned = sem("xn_turned")
        xnT_ready = sem("xnT_ready")
        h_done = sem("h_done")
        h_copied = sem("h_copied")
        h_stored = sem("h_stored")
        src_stored = sem("src_stored")
        table_ready = sem("table_ready")
        table_stored = sem("table_stored")
        table_back = sem("table_back")
        floats_ready = sem("floats_ready")
        cols_turned = sem("cols_turned")
        cols_taken = sem("cols_taken")
        src_b_in = [sem(f"src_b_in{q}") for q in range(GB)]
        h_in = [sem(f"h_in{q}") for q in range(GB)]
        gathered = sem("gathered")
        rows_ready = sem("rows_ready")
        dst_ready = sem("dst_ready")
        pick_ready = sem("pick_ready")
        mixed = sem("mixed")
        mix_ready = sem("mix_ready")
        summed = sem("summed")
        msg_ready = sem("msg_ready")
        added = [sem(f"added{c}") for c in range(COPIES)]

        with nc.Block() as block:
            @block.sync
            def _(sp):
                sp.dma_start(w_rows[:], gnn_w.rearrange("(b p) d -> p b d", p=P)).then_inc(w_in, 16)
                for t in range(WT - 1):
                    sp.dma_start(x1[:, t * WB:(t + 1) * WB, :],
                                 x[t * WB * P:(t + 1) * WB * P, :].rearrange("(w p) d -> p w d", p=P)).then_inc(x_in[t], 16)
                sp.wait_ge(pads_set, 1)
                w0 = (WT - 1) * WB
                sp.dma_start(x1[:, w0:NW - 1, :],
                             x[w0 * P:(NW - 1) * P, :].rearrange("(w p) d -> p w d", p=P)).then_inc(x_in[WT - 1], 16)
                sp.dma_start(x1[0:LASTW, NW - 1, :], x[(NW - 1) * P:N, :]).then_inc(x_in[WT - 1], 16)
                sp.wait_ge(pads_set, 4)
                for rows, given in ((src_rows, src), (dst_rows, dst), (wgt_rows, edge_weight)):
                    sp.dma_start(rows[0:FULL, :], given[0:FULL * GE].rearrange("(g e) -> g e", e=GE)).then_inc(edges_in, 16)
                    sp.dma_start(rows[FULL:FULL + 1, 0:REST], given[FULL * GE:NE].rearrange("(g e) -> g e", g=1)).then_inc(edges_in, 16)
                sp.wait_ge(edges_in, 96)
                sp.dma_start(src_dram, src_rows[:]).then_inc(src_stored, 16)
                sp.wait_ge(table_ready, 1)
                sp.dma_start(table_dram, table[:]).then_inc(table_stored, 16)
                sp.wait_ge(table_stored, 16)
                sp.dma_start(table_b[:], table_dram.partition_broadcast(P)).then_inc(table_back, 16)
                sp.dma_start(gate_sb[:], gate_w.rearrange("(b p) e -> p b e", p=P)).then_inc(later_in, 16)
                sp.dma_start(gate_bb[:], gate_b.partition_broadcast(P)).then_inc(later_in, 16)
                sp.dma_start(b1_rows[:], b1.rearrange("e (b p) -> (e b) p", p=P)).then_inc(b1_in, 16)
                sp.dma_start(b2_b[:], b2.partition_broadcast(P)).then_inc(later_in, 16)
                sp.dma_start(gamma_b[:], gamma.partition_broadcast(P)).then_inc(later_in, 16)
                sp.dma_start(beta_b[:], beta.partition_broadcast(P)).then_inc(later_in, 16)
                for t in range(WT):
                    sp.wait_ge(h_copied, (t + 1) * WB)
                    sp.dma_start(h_rows_dram[t * WB * P:(t + 1) * WB * P, :].rearrange("(w p) d -> p w d", p=P),
                                 h_stage[:]).then_inc(h_stored, 16)
                sp.wait_ge(h_stored, 16 * WT)
                sp.wait_ge(src_stored, 16)
                sp.wait_ge(later_in, 16 * 5)

            @block.gpsimd
            def _(pool):
                link = Chain(pool, pool_own)
                pool.memset(x1[:, NW - 1, :], 0.0).then_inc(pads_set, 1)
                pool.memset(src_rows[:], 0).then_inc(pads_set, 1)
                pool.memset(dst_rows[:], N - 1).then_inc(pads_set, 1)
                pool.memset(wgt_rows[:], 0.0).then_inc(pads_set, 1)
                pool.memset(zeros[:], 0.0).then_inc(zero_set, 1)
                link(pool.memset(ident[:], 0.0))
                pool.affine_select(out=ident[:], in_=ident[:], compare_op=ALU.not_equal, fill=1.0, base=0,
                                   pattern=[[-1, P]], channel_multiplier=1).then_inc(consts, 1)
                link(pool.memset(ones[:], 1.0))
                pool.affine_select(out=before[:], in_=ones[:], compare_op=ALU.is_gt, fill=0.0, base=0,
                                   pattern=[[-1, P]], channel_multiplier=1).then_inc(consts, 1)
                pool.memset(ones_b[:], 1.0).then_inc(consts, 1)
                pool.affine_select(out=upper_f[:], in_=ones[:], compare_op=ALU.is_gt, fill=0.0, base=0,
                                   pattern=[[1, P]], channel_multiplier=-1).then_inc(consts, 1)
                pool.iota(iota_i[:], [[1, P]], base=0, channel_multiplier=0).then_inc(consts, 1)
                pool.iota(part_i[:], [[0, 1]], base=0, channel_multiplier=1).then_inc(consts, 1)
                pool.memset(eps[:], EPS).then_inc(consts, 1)

            @block.scalar
            def _(act):
                act.dma_start(acc[0][0:(NW - 1) * P, :].rearrange("(p a) d -> p (a d)", p=P),
                              x[0:(NW - 1) * P, :].rearrange("(p a) d -> p (a d)", p=P)).then_inc(acc_init, 16)
                act.dma_start(acc[0][(NW - 1) * P:N, :], x[(NW - 1) * P:N, :]).then_inc(acc_init, 16)
                act.wait_ge(zero_set, 1)
                act.dma_start(acc[0][N:NP, :], zeros[0:NP - N, 0:D]).then_inc(acc_init, 16)
                act.dma_start(acc[0][NP:ROWS, :], zeros[:, 0:D]).then_inc(acc_init, 16)
                A = ROWS // P
                for c in range(1, COPIES):
                    rows = acc[c].rearrange("(p a) d -> p (a d)", p=P)
                    for a in range(0, A, 10):
                        act.dma_start(rows[:, a * D:(a + 10) * D], zeros[:]).then_inc(acc_init, 16)
                act.wait_ge(consts, 7)
                def copy_h(w):
                    if w % WB == 0 and w >= WB:
                        act.wait_ge(h_stored, 16 * (w // WB))
                    act.wait_ge(h_done, w + 1)
                    act.activation(h_stage[:, w % WB, :], bk[4 + w % 2][:, 0:D], ACT.Copy).then_inc(h_copied, 1)

                act.wait_ge(mv_ready, 1)
                act.activation(std[:], mv[:, :, 1], ACT.Sqrt, bias=eps[:]).then_inc(std_ready, 1)
                act.wait_ge(shift_ready, 1)
                for w in range(NW):
                    if w >= WB:
                        act.wait_ge(xn_turned, w - WB + 1)
                    act.activation(xn[:, w % WB, :], x1[:, w, :], ACT.Identity, bias=shift[:, w:w + 1],
                                   scale=rstd[:, w:w + 1]).then_inc(xn_ready, 1)
                    if w >= WB:
                        copy_h(w - WB)
                for w in range(NW - WB, NW):
                    copy_h(w)
                act.wait_ge(acc_init, 16 * (4 + (COPIES - 1) * A // 10))

            @block.vector
            def _(dve):
                link = Chain(dve, dve_own)
                v = nc.vector

                dve.wait_ge(consts, 7)
                link(v.tensor_copy(iota_f[:], iota_i[:]))
                v.tensor_copy(upper[:], upper_f[:])
                link(v.tensor_copy(part_f[:], part_i[:]))
                link(v.tensor_scalar(junk_row[:], part_f[:], float(JUNK), None, ALU.add))
                dve.wait_ge(edges_in, 96)
                link(v.tensor_copy(dst_rf[:], dst_rows[:]))
                v.tensor_reduce(lohi[:, 0:1], dst_rf[:], AX.X, ALU.min)
                link(v.tensor_reduce(lohi[:, 1:2], dst_rf[:], AX.X, ALU.max))
                link(v.tensor_scalar(table[:, 0:1], lohi[:, 0:1], float(NP - P), None, ALU.min))
                link(v.tensor_tensor(span[:], lohi[:, 1:2], table[:, 0:1], ALU.subtract))
                v.tensor_scalar(table[:, 1:2], span[:], float(P - 1), None, ALU.is_gt).then_inc(table_ready, 1)
                v.tensor_copy(src_rf[:], src_rows[:]).then_inc(floats_ready, 1)
                for w in range(NW):
                    if w % WB == 0:
                        dve.wait_ge(x_in[w // WB], 16 + 16 * (w // WB == WT - 1))
                    s = v.bn_stats(stats[:, w, :], x1[:, w, :])
                link(s)
                for w in range(NW):
                    s = v.bn_aggr(mv[:, w, :], stats[:, w, :])
                s.then_inc(mv_ready, 1)
                for b in range(NB):
                    dve.wait_ge(w_t, b + 1)
                    v.tensor_copy(wT[:, b, :], bk[b][:, 0:D]).then_inc(wT_ready, 1)
                dve.wait_ge(std_ready, 1)
                link(v.reciprocal(rstd[:], std[:]))
                v.scalar_tensor_tensor(shift[:], mv[:, :, 0], -1.0, rstd[:], ALU.mult, ALU.mult).then_inc(shift_ready, 1)
                for w in range(NW):
                    dve.wait_ge(xn_turned, w + 1)
                    if w >= 2:
                        dve.wait_ge(h_done, w - 1)
                    v.tensor_copy(xnT[:, w % 2, :, :], bk[w % 2][:, 0:D].rearrange("p (b n) -> p b n", b=NB)).then_inc(xnT_ready, 1)
                dve.wait_ge(b1_turned, 1)
                v.tensor_copy(b1_cols[:], bk[2][:, 0:EX * FB])
                dve.wait_ge(cols_turned, 1)
                for n, field in enumerate((SRC, DST, WGT)):
                    for half in range(2):
                        dve.wait_ge(cols_turned, 2 * n + half + 1)
                        s = v.tensor_copy(cols[:, :, field, 4 * half:4 * half + 4],
                                          bk[6 + half][:, 0:4 * NG].rearrange("p (j g) -> p g j", j=4))
                        s.then_inc(cols_taken, 1)
                dve.wait_ge(cols_taken, 6)
                dve.wait_ge(table_back, 16)
                lo = table_b[:, :, 0:1].to_broadcast([P, NG, GT])
                slow = table_b[:, :, 1:2].to_broadcast([P, NG, GT])
                rel, off = cols[:, :, REL, :], cols[:, :, OFF, :]
                v.tensor_scalar(off, cols[:, :, SRC, :], junk_row[:], None, ALU.subtract)
                v.tensor_copy(table_i[:], table_b[0:1, :, :].rearrange("p g c -> p (g c)"))
                link(v.tensor_copy(slow_f[:], table_b[0:1, :, 1:2].rearrange("p g c -> p (g c)")))
                link(v.tensor_tensor_scan(slows_f[:], ones[0:1, 0:NG], slow_f[:], 0.0, ALU.mult, ALU.add))
                v.tensor_scalar(gathers_i[:], slows_f[:], 16.0 * GT, None, ALU.mult)
                link(v.tensor_tensor(rel, cols[:, :, DST, :], lo, ALU.subtract))
                link(v.tensor_scalar(rel, rel, part_f[:], None, ALU.subtract))
                link(v.tensor_scalar(table_b[:, :, 1:2], table_b[:, :, 1:2], -1.0, 1.0, ALU.mult, ALU.add))
                link(v.tensor_tensor(rel, rel, slow, ALU.mult))
                link(v.tensor_scalar(rel, rel, part_f[:], None, ALU.add))

            @block.tensor
            def _(pe):
                pe.wait_ge(consts, 7)
                pe.wait_ge(w_in, 16)
                for b in range(NB):
                    for a in range(NB):
                        s = nc.tensor.transpose(bk[b][:, a * P:(a + 1) * P], w_rows[:, a, b * P:(b + 1) * P], ident[:])
                    s.then_inc(w_t, 1)
                pe.wait_ge(wT_ready, NB)

                def turn_window(w):
                    pe.wait_ge(xn_ready, w + 1)
                    if w >= 2:
                        pe.wait_ge(xnT_ready, w - 1)
                    for b in range(NB):
                        s = nc.tensor.transpose(bk[w % 2][:, b * P:(b + 1) * P], xn[:, w % WB, b * P:(b + 1) * P], ident[:])
                    s.then_inc(xn_turned, 1)

                turn_window(0)
                for w in range(NW):
                    if w + 1 < NW:
                        turn_window(w + 1)
                    pe.wait_ge(xnT_ready, w + 1)
                    if w >= 2:
                        pe.wait_ge(h_copied, w - 1)
                    for b in range(NB):
                        s = nc.tensor.matmul(bk[4 + w % 2][:, 0:D], xnT[:, w % 2, b, :], wT[:, b, :],
                                             start=b == 0, stop=b == NB - 1)
                    s.then_inc(h_done, 1)
                pe.wait_ge(b1_in, 16)
                nc.tensor.transpose(bk[2][:, 0:EX * FB], b1_rows[:], ident[0:EX * FB, 0:EX * FB]).then_inc(b1_turned, 1)
                pe.wait_ge(floats_ready, 1)
                for n, rows in enumerate((src_rf, dst_rf, wgt_rows)):
                    for half in range(2):
                        if n > 0:
                            pe.wait_ge(cols_taken, 2 * n + half - 1)
                        for j in range(4):
                            e = (4 * half + j) * P
                            s = nc.tensor.transpose(bk[6 + half][:, j * NG:(j + 1) * NG], rows[:, e:e + P], ident[0:NG, 0:NG])
                        s.then_inc(cols_turned, 1)

        prepare.close()

        def sb(name, shape, dt):
            return layer1.enter_context(nc.sbuf_tensor(name, shape, dt))

        cols_s = sb("cols_s", [P, GB, 5, GT], fp32)
        src_b = sb("src_b", [P, GB, GE], i32)
        h_buf = sb("h_buf", [P, GB, GT, D], fp32)
        dup = sb("dup", [P, GB, GT], fp32)
        row_f = sb("row_f", [P, GB, GT], fp32)
        row_i = sb("row_i", [P, GB, GT], i32)
        dst_i = sb("dst_i", [P, GB, GT], i32)
        merge = sb("merge", [P, GB, GT, P], fp32)
        pick = sb("pick", [P, GB, GT, P], fp32)
        mix = sb("mix", [P, 2, 2, P], fp32)
        msg = sb("msg", [P, 4, 2, D], fp32)

        def turns(engine, body):
            body(0)
            with engine.Fori(1, GTURNS) as i:
                body(i)

        with nc.Block() as block:
            @block.sync
            def _(sp):
                def body(i):
                    for q in range(GB):
                        await_turn(sp, pick_ready, i, GB * GT, GT * (q + 1) - GB * GT)
                        sp.dma_start(src_b[:, q, :], src_dram[ds(i * GB + q, 1), :].to_broadcast([P, GE])).then_inc(src_b_in[q], 16)
                        slow = sp.value_load(table_i[0:1, ds(i * (2 * GB) + (2 * q + 1), 1)], min_val=0, max_val=1)
                        lo = sp.value_load(table_i[0:1, ds(i * (2 * GB) + 2 * q, 1)], min_val=0, max_val=NP - P)
                        await_turn(sp, summed, i, PT, PAIRS * (q + 1) - PT)
                        sp.sem_inc(sp_steps, 1)
                        with sp.If(slow == 0):
                            sp.dma_start(h_buf[:, q, 0, :], h_rows_dram[ds(lo, P), :]).then_inc(h_in[q], 16)
                        sp.nop()
                turns(sp, body)

            @block.gpsimd
            def _(pool):
                def settled():
                    pool.sem_inc(pool_steps, 1)

                def body(i):
                    for q in range(GB):
                        pool.wait_ge(dst_ready, i * GB + (q + 1))
                        slow = pool.value_load(table_i[0:1, ds(i * (2 * GB) + (2 * q + 1), 1)], min_val=0, max_val=1)
                        with pool.If(slow == 1):
                            await_turn(pool, summed, i, PT, PAIRS * (q + 1) - PT)
                            settled()
                            for j in range(GT):
                                pool.indirect_dma_start(h_buf[:, q, j, :], None, h_rows_dram,
                                                        bass.IndirectOffsetOnAxis(ap=dst_i[:, q, j:j + 1], axis=0)).then_inc(gathered, 16)
                            pool.wait_ge(gathered, pool.value_load(gathers_i[0:1, ds(i * GB + q, 1)], min_val=16 * GT, max_val=16 * GT * NG))
                            pool.sem_inc(h_in[q], 16)
                        pool.wait_ge(rows_ready, i * GB + (q + 1))
                        for j in range(GT):
                            u = q * GT + j
                            c = u % COPIES
                            if j % 2 == 0:
                                pool.wait_ge(msg_ready, i * PT + (u // 2 + 1))
                            per = 16 * GB * GT // COPIES
                            await_turn(pool, added[c], i, per, 16 * (u // COPIES))
                            settled()
                            pool.indirect_dma_start(acc[c], bass.IndirectOffsetOnAxis(ap=row_i[:, q, j:j + 1], axis=0),
                                                    msg[:, (u // 2) % 4, j % 2, :], None,
                                                    compute_op=ALU.add).then_inc(added[c], 16)
                turns(pool, body)
                for c in range(COPIES):
                    pool.wait_ge(added[c], 16 * NG * GT // COPIES)

            @block.vector
            def _(dve):
                link = Chain(dve, dve_step)
                v = nc.vector

                def body(i):
                    link.enter(i, 3 * GB)
                    for q in range(GB):
                        link(v.tensor_copy(cols_s[:, q, :, :], cols[:, ds(i * GB + q, 1), :, :].rearrange("p g f j -> p (g f) j")))
                        await_turn(dve, summed, i, PT, PAIRS * (q + 1) - PT)
                        v.tensor_copy(dst_i[:, q, :], cols_s[:, q, DST, :]).then_inc(dst_ready, 1)
                        await_turn(dve, mixed, i, PT, PAIRS * (q + 1) - PT)
                        dve.wait_ge(src_b_in[q], i * 16 + 16)
                        for j in range(GT):
                            s = v.scalar_tensor_tensor(merge[:, q, j, :], src_b[:, q, j * P:(j + 1) * P], cols_s[:, q, SRC, j:j + 1], before[:],
                                                       ALU.is_equal, ALU.mult, accum_out=dup[:, q, j:j + 1])
                        link(s)
                        for j in range(GT):
                            v.tensor_scalar(merge[:, q, j, :], src_b[:, q, j * P:(j + 1) * P], cols_s[:, q, SRC, j:j + 1],
                                            cols_s[:, q, WGT, j:j + 1], ALU.is_equal, ALU.mult)
                            v.tensor_scalar(pick[:, q, j, :], iota_f[:], cols_s[:, q, REL, j:j + 1], None,
                                            ALU.is_equal).then_inc(pick_ready, 1)
                        link(v.scalar_tensor_tensor(row_f[:, q, :], dup[:, q, :], 0.0, cols_s[:, q, OFF, :], ALU.is_equal, ALU.mult))
                        for c in range(COPIES):
                            per = 16 * GB * GT // COPIES
                            await_turn(dve, added[c], i, per, 16 * GT // COPIES * (q + 1) - per)
                        v.tensor_scalar(row_i[:, q, :], row_f[:, q, :], junk_row[:], None, ALU.add).then_inc(rows_ready, 1)
                turns(dve, body)

            @block.tensor
            def _(pe):
                def sums(i, k, slow):
                    q = k // PAIRS
                    if k % PAIRS == 0:
                        pe.wait_ge(h_in[q], i * 16 + 16)
                    pe.wait_ge(mix_ready, i * PT + (k + 1))
                    await_turn(pe, msg_ready, i, PT, k + 1 - 4)
                    for e in range(2):
                        j = (2 * k + e) % GT
                        s = nc.tensor.matmul(bk[2 + k % 4][:, e * D:(e + 1) * D], mix[:, k % 2, e, :],
                                             h_buf[:, q, ds(slow * j, 1), :].rearrange("p j d -> p (j d)"), start=True, stop=True)
                    s.then_inc(summed, 1)


                def body(i):
                    prev = i - 1
                    slow = None
                    for k in range(PT):
                        q = k // PAIRS
                        pe.wait_ge(pick_ready, i * (GB * GT) + (2 * k + 2))
                        await_turn(pe, mix_ready, i, PT, k + 1 - 2)
                        for e in range(2):
                            j = (2 * k + e) % GT
                            s = nc.tensor.matmul(bk[k % 2][:, e * P:(e + 1) * P], pick[:, q, j, :], merge[:, q, j, :], start=True, stop=True)
                        s.then_inc(mixed, 1)
                        if k == 0:
                            if isinstance(i, int):
                                pass
                            else:
                                sl = pe.value_load(table_i[0:1, ds(i * (2 * GB) - 1, 1)], min_val=0, max_val=1)
                                sums(prev, PT - 1, sl)
                        else:
                            if (k - 1) % PAIRS == 0:
                                slow = pe.value_load(table_i[0:1, ds(i * (2 * GB) + (2 * ((k - 1) // PAIRS) + 1), 1)], min_val=0, max_val=1)
                            sums(i, k - 1, slow)
                turns(pe, body)
                sl = pe.value_load(table_i[0:1, 2 * NG - 1:2 * NG], min_val=0, max_val=1)
                sums(GTURNS - 1, PT - 1, sl)

            @block.scalar
            def _(act):
                def take_msg(i, k):
                    act.wait_ge(summed, i * PT + (k + 1))
                    for c in ((2 * k) % COPIES, (2 * k + 1) % COPIES):
                        per = 16 * GB * GT // COPIES
                        await_turn(act, added[c], i, per, 16 * ((2 * k - 8) // COPIES + 1))
                    act.activation(msg[:, k % 4, :, :], bk[2 + k % 4][:, 0:2 * D].rearrange("p (e d) -> p e d", e=2),
                                   ACT.Copy).then_inc(msg_ready, 1)

                def body(i):
                    for k in range(PT):
                        act.wait_ge(mixed, i * PT + (k + 1))
                        await_turn(act, summed, i, PT, k + 1 - 2)
                        act.activation(mix[:, k % 2, :, :], bk[k % 2][:, 0:2 * P].rearrange("p (e m) -> p e m", e=2),
                                       ACT.Copy).then_inc(mix_ready, 1)
                        if k > 0:
                            take_msg(i, k - 1)
                        elif not isinstance(i, int):
                            take_msg(i - 1, PT - 1)
                turns(act, body)
                take_msg(GTURNS - 1, PT - 1)

        layer1.close()

        def window_turns(engine, body):
            body(0, 0)
            with engine.Fori(0, (WT - 1) // 2) as i:
                body(i * 2 + 1, 1)
                body(i * 2 + 2, 0)

        gate_stage = ctx.enter_context(ExitStack())

        def sb(name, shape, dt):
            return gate_stage.enter_context(nc.sbuf_tensor(name, shape, dt))

        WD = WB * D
        K2 = 2 * WB
        parts = [sb(f"part{c}", [P, WB, D], fp32) for c in range(1, COPIES)]
        stats2 = sb("stats2", [P, WB, 6], fp32)
        mv2 = sb("mv2", [P, WB, 2], fp32)
        std2 = sb("std2", [P, WB], fp32)
        rs = sb("rs", [P, WB], fp32)
        sh = sb("sh", [P, WB], fp32)
        xr = [sb(f"xr{q}", [P, WB, RW], fp32) for q in range(2)]
        xrT = sb("xrT", [P, 2, NB, P], fp32)
        logits = sb("logits", [P, WB, EX], fp32)
        top8 = sb("top8", [P, WB, 8], fp32)
        idx8 = sb("idx8", [P, WB, 8], u32)
        choice = sb("choice", [P, WB, 2], fp32)
        hot_f = sb("hot_f", [P, K2, EX], fp32)
        hot = sb("hot", [P, K2, EX], bf16)
        hot_sum = sb("hot_sum", [P, EX], fp32)
        ranks = sb("ranks", [P, K2, EX], fp32)
        slot_f = sb("slot_f", [P, K2], fp32)
        slot_i = sb("slot_i", [P, 2, K2], i32)
        gap = sb("gap", [P, NW], fp32)
        ratio = sb("ratio", [P, NW], fp32)
        total = sb("total", [P, NW], fp32)

        x1_in = [sem(f"x1_in{c}") for c in range(COPIES)]
        x1_summed = sem("x1_summed")
        mv2_ready = sem("mv2_ready")
        std2_ready = sem("std2_ready")
        norm2_ready = sem("norm2_ready")
        xr_ready = sem("xr_ready")
        xr_turned = sem("xr_turned")
        xrT_ready = sem("xrT_ready")
        gated = sem("gated")
        logits_taken = sem("logits_taken")
        hot_ready = sem("hot_ready")
        ranked = sem("ranked")
        slots_ready = sem("slots_ready")
        sent = [sem(f"sent{q}") for q in range(2)]
        gate_own = sem("gate_own")
        counted = sem("counted")
        counts_ready = sem("counts_ready")
        tiles_ready = sem("tiles_ready")
        fill_set = sem("fill_set")
        filled = sem("filled")
        gap_ready = sem("gap_ready")
        ratio_ready = sem("ratio_ready")

        with nc.Block() as block:
            @block.sync
            def _(sp):
                def body(t, q):
                    await_turn(sp, x1_summed, t, 1, 0)
                    for c in range(COPIES):
                        to = x1[:, ds(t * WB, WB), :] if c == 0 else parts[c - 1][:]
                        sp.dma_start(to, acc[c][ds(t * (WB * P), WB * P), :].rearrange("(w p) d -> p w d", p=P)).then_inc(x1_in[c], 16)
                window_turns(sp, body)
                sp.wait_ge(counts_ready, 1)
                with sp.Fori(0, EX) as e:
                    count = sp.value_load(counts_i[0:1, ds(e, 1)], min_val=0, max_val=NP)
                    sp.dma_start(slots_dram[ds(e * CAP + count, P), :], filler[:]).then_inc(filled, 16)
                sp.wait_ge(filled, 16 * EX)

            @block.gpsimd
            def _(pool):
                def body(t, q):
                    pool.wait_ge(slots_ready, t + 1)
                    pool.sem_inc(pool_steps, 1)
                    for n in range(K2):
                        pool.indirect_dma_start(slots_dram, bass.IndirectOffsetOnAxis(ap=slot_i[:, q, n:n + 1], axis=0),
                                                xr[q][:, n // 2, :], None).then_inc(sent[q], 16)
                window_turns(pool, body)
                pool.wait_ge(sent[0], 16 * K2 * ((WT + 1) // 2))
                pool.wait_ge(sent[1], 16 * K2 * (WT // 2))

            @block.scalar
            def _(act):
                def body(t, q):
                    act.wait_ge(mv2_ready, t + 1)
                    act.activation(std2[:], mv2[:, :, 1], ACT.Sqrt, bias=eps[:]).then_inc(std2_ready, 1)
                    if q == 0:
                        await_turn(act, sent[0], t, 8 * K2, 0)
                    else:
                        await_turn(act, sent[1], t, 8 * K2, -8 * K2)
                    act.wait_ge(norm2_ready, t + 1)
                    for j in range(WB):
                        act.activation(xr[q][:, j, 0:D], x1[:, ds(t * WB + j, 1), :].rearrange("p w d -> p (w d)"),
                                       ACT.Identity, bias=sh[:, j:j + 1], scale=rs[:, j:j + 1]).then_inc(xr_ready, 1)
                    for j in range(WB):
                        act.wait_ge(xr_turned, t * WB + (j + 1))
                        await_turn(act, gated, t, WB, j - 1)
                        act.activation(xrT[:, j % 2, :, :], bk[j % 2][:, 0:D].rearrange("p (b n) -> p b n", b=NB),
                                       ACT.Copy).then_inc(xrT_ready, 1)
                window_turns(act, body)
                act.wait_ge(gap_ready, 1)
                act.activation(ratio[:], gap[:], ACT.Exp).then_inc(ratio_ready, 1)

            @block.tensor
            def _(pe):
                def turn_window(t, q, j):
                    pe.wait_ge(xr_ready, t * WB + (j + 1))
                    await_turn(pe, xrT_ready, t, WB, j - 1)
                    for b in range(NB):
                        s = nc.tensor.transpose(bk[j % 2][:, b * P:(b + 1) * P], xr[q][:, j, b * P:(b + 1) * P], ident[:])
                    s.then_inc(xr_turned, 1)

                def body(t, q):
                    await_turn(pe, logits_taken, t, 1, 0)
                    turn_window(t, q, 0)
                    for j in range(WB):
                        if j + 1 < WB:
                            turn_window(t, q, j + 1)
                        pe.wait_ge(xrT_ready, t * WB + (j + 1))
                        for b in range(NB):
                            s = nc.tensor.matmul(bk[2][:, j * EX:(j + 1) * EX], xrT[:, j % 2, b, :], gate_sb[:, b, :],
                                                 start=b == 0, stop=b == NB - 1)
                        s.then_inc(gated, 1)
                    pe.wait_ge(hot_ready, t + 1)
                    nc.tensor.matmul(bk[3][:, 0:K2 * EX], upper[:], hot[:].rearrange("p n e -> p (n e)"),
                                     start=True, stop=False, skip_group_check=True)
                    for n in range(1, K2):
                        nc.tensor.matmul(bk[3][:, n * EX:K2 * EX], ones_b[:], hot[:, 0:K2 - n, :].rearrange("p n e -> p (n e)"),
                                         start=False, stop=False, skip_group_check=True)
                    nc.tensor.matmul(bk[3][:, 0:K2 * EX].rearrange("p (n e) -> p n e", e=EX), ones_b[:],
                                     carry[:, None, :].to_broadcast([P, K2, EX]),
                                     start=False, stop=True, skip_group_check=True).then_inc(ranked, 1)
                window_turns(pe, body)
                pe.wait_ge(counted, 1)
                nc.tensor.matmul(bk[4][0:1, 0:EX], ones_b[:, 0:1], carry[:], start=True, stop=True).then_inc(counted, 1)

            @block.vector
            def _(dve):
                link = Chain(dve, gate_own)
                v = nc.vector

                def body(t, q):
                    link.enter(t, 17)
                    here = x1[:, ds(t * WB, WB), :]
                    for c in range(1, COPIES):
                        dve.wait_ge(x1_in[c], t * 16 + 16)
                        if c == 1:
                            dve.wait_ge(x1_in[0], t * 16 + 16)
                        s = v.tensor_tensor(here, here, parts[c - 1][:], ALU.add)
                        link(s)
                    dve.sem_inc(x1_summed, 1)
                    for j in range(WB):
                        s = v.bn_stats(stats2[:, j, :], x1[:, ds(t * WB + j, 1), :].rearrange("p w d -> p (w d)"))
                    link(s)
                    dve.sem_inc(dve_steps, 1)
                    for j in range(WB):
                        s = v.bn_aggr(mv2[:, j, :], stats2[:, j, :])
                    s.then_inc(mv2_ready, 1)
                    dve.wait_ge(std2_ready, t + 1)
                    await_turn(dve, xr_ready, t, WB, 0)
                    link(v.reciprocal(rs[:], std2[:]))
                    link(v.scalar_tensor_tensor(sh[:], mv2[:, :, 0], -1.0, rs[:], ALU.mult, ALU.mult))
                    v.tensor_copy(rstd2[:, ds(t * WB, WB)], rs[:])
                    v.tensor_copy(shift2[:, ds(t * WB, WB)], sh[:]).then_inc(norm2_ready, 1)
                    dve.wait_ge(gated, t * WB + WB)
                    s = v.tensor_tensor(logits[:], bk[2][:, 0:WB * EX].rearrange("p (w e) -> p w e", e=EX),
                                        gate_bb[:, None, :].to_broadcast([P, WB, EX]), ALU.add)
                    link(s)
                    dve.sem_inc(logits_taken, 1)
                    for j in range(WB):
                        s = v.max(top8[:, j, :], logits[:, j, :])
                    link(s)
                    dve.sem_inc(dve_steps, 1)
                    for j in range(WB):
                        s = v.max_index(idx8[:, j, :], top8[:, j, :], logits[:, j, :])
                    link(s)
                    v.tensor_copy(top2[:, ds(t * WB, WB), :], top8[:, :, 0:2])
                    link(v.tensor_copy(choice[:], idx8[:, :, 0:2]))
                    for k in range(2):
                        s = v.tensor_tensor(hot_f[:].rearrange("p (w k) e -> p w k e", k=2)[:, :, k, :],
                                            iota_f[:, None, 0:EX].to_broadcast([P, WB, EX]),
                                            choice[:, :, k:k + 1].to_broadcast([P, WB, EX]), ALU.is_equal)
                    link(s)
                    v.tensor_reduce(hot_sum[:], hot_f[:].rearrange("p n e -> p e n"), AX.X, ALU.add)
                    link(v.tensor_copy(hot[:], hot_f[:]))
                    dve.sem_inc(hot_ready, 1)
                    dve.wait_ge(ranked, t + 1)
                    link(v.tensor_tensor(ranks[:], bk[3][:, 0:K2 * EX].rearrange("p (n e) -> p n e", e=EX),
                                         expert_base[:, None, :].to_broadcast([P, K2, EX]), ALU.add))
                    link(v.tensor_tensor(ranks[:], ranks[:], hot_f[:], ALU.mult))
                    v.tensor_tensor(carry_f[:], carry_f[:], hot_sum[:], ALU.add)
                    link(v.tensor_reduce(slot_f[:], ranks[:], AX.X, ALU.add))
                    v.tensor_copy(carry[:], carry_f[:])
                    v.tensor_copy(xr[q][:, :, TOKEN], tok[:])
                    v.tensor_copy(xr[q][:, :, CHOICE], choice[:, :, 0])
                    link(v.tensor_copy(slot_i[:, q, :], slot_f[:]))
                    link(v.tensor_scalar(tok[:], tok[:], float(WB * P), None, ALU.add))
                    dve.sem_inc(slots_ready, 1)
                for q in range(2):
                    v.memset(xr[q][:, :, D:RW], 0.0)
                v.memset(carry_f[:], 0.0)
                v.memset(carry[:], 0.0)
                link(v.memset(filler[:], 0.0))
                for j in range(WB):
                    v.tensor_scalar(tok[:, j:j + 1], part_f[:], float(j * P), None, ALU.add)
                v.tensor_scalar(expert_base[:], iota_f[:, 0:EX], float(CAP), None, ALU.mult)
                v.tensor_scalar(filler[:, TOKEN:TOKEN + 1], part_f[:], float(NP), None, ALU.add)
                link(v.memset(filler[:, CHOICE:CHOICE + 1], -1.0))
                window_turns(dve, body)
                link.leave(WT)
                dve.sem_inc(counted, 1)
                dve.wait_ge(counted, 2)
                link(v.tensor_copy(counts_f[:], bk[4][0:1, 0:EX]))
                v.tensor_copy(counts_i[:], counts_f[:]).then_inc(counts_ready, 1)
                link(v.tensor_scalar(ntiles_i[:], counts_f[:], float(P - 1), None, ALU.add))
                link(v.tensor_scalar(ntiles_i[:], ntiles_i[:], P.bit_length() - 1, None, ALU.arith_shift_right))
                link(v.tensor_scalar(ntiles_f[:], ntiles_i[:], 1.0, None, ALU.max))
                link(v.tensor_tensor_scan(ends_f[:], ones[0:1, 0:EX], ntiles_f[:], 0.0, ALU.mult, ALU.add))
                v.memset(tiles_i[:, 0:1], 0)
                link(v.tensor_copy(tiles_i[:, 1:EX + 1], ends_f[:]))
                v.tensor_tensor(gap[:], top2[:, :, 1], top2[:, :, 0], ALU.subtract).then_inc(gap_ready, 1)
                dve.wait_ge(ratio_ready, 1)
                link(v.tensor_scalar(total[:], ratio[:], 1.0, None, ALU.add))
                link(v.reciprocal(first_w[:], total[:]))
                link(v.tensor_tensor(second_w[:], ratio[:], first_w[:], ALU.mult))
        gate_stage.close()

        expert_stage = ctx.enter_context(ExitStack())

        def sb(name, shape, dt):
            return expert_stage.enter_context(nc.sbuf_tensor(name, shape, dt))

        xt = sb("xt", [P, RW], fp32)
        xtT = sb("xtT", [P, NB, P], fp32)
        held = sb("held", [P, 2], fp32)
        other = sb("other", [P, 1], fp32)
        to_i = sb("to_i", [P, 1], i32)
        hT = sb("hT", [P, FB, P], fp32)
        y_sb = sb("y_sb", [P, D], fp32)

        xt_in = sem("xt_in")
        xt_turned = sem("xt_turned")
        xt_read = sem("xt_read")
        xtT_ready = sem("xtT_ready")
        up_done = sem("up_done")
        hT_ready = sem("hT_ready")
        down_done = sem("down_done")
        y_ready = sem("y_ready")
        y_sent = sem("y_sent")
        first_set = sem("first_set")
        w1_in = [sem(f"w1_in{q}") for q in range(2)]
        expert_own = sem("expert_own")

        def load_expert(engine, e, q):
            engine.dma_start(w1_sb[:, q, :, :], w1[ds(e, 1), :, :].rearrange("e (b p) f -> p (e b) f", p=P)).then_inc(w1_in[q], 16)
            engine.dma_start(w2_sb[:, q, :, :], w2[ds(e, 1), :, :].rearrange("e (b p) d -> p (e b) d", p=P)).then_inc(w1_in[q], 16)

        def experts(engine, start, tile, end):
            with engine.Fori(0, EX // 2) as i:
                for q in range(2):
                    e = i * 2 + q
                    lo = engine.value_load(tiles_i[0:1, ds(e, 1)], min_val=0, max_val=MAXT)
                    hi = engine.value_load(tiles_i[0:1, ds(e + 1, 1)], min_val=1, max_val=MAXT)
                    start(i, e, q)
                    with engine.Fori(lo, hi) as s:
                        tile(i, e, q, s, lo)
                    end(i, e, q, hi)

        MAXT = 2 * NP // P + EX

        def nothing(*_):
            pass

        with nc.Block() as block:
            @block.sync
            def _(sp):
                def tile(i, e, q, s, lo):
                    sp.wait_ge(xt_turned, s + 1)
                    sp.wait_ge(xt_read, s + 1)
                    sp.dma_start(xt[:], slots_dram[ds((e * CAP + (s - lo) * P).with_bounds(min_val=0, max_val=EX * CAP - P), P), :]).then_inc(xt_in, 16)

                def end(i, e, q, hi):
                    pass
                experts(sp, nothing, tile, end)
                tiles = sp.value_load(tiles_i[0:1, EX:EX + 1], min_val=EX, max_val=MAXT)
                sp.wait_ge(xt_turned, tiles + 1)
                sp.wait_ge(xt_read, tiles + 1)
                sp.dma_start(xt[:], slots_dram[0:P, :]).then_inc(xt_in, 16)
                sp.wait_ge(xt_in, tiles * 16 + 16)
                sp.sem_inc(sp_steps, 1)

            @block.gpsimd
            def _(pool):
                def scatter():
                    pool.indirect_dma_start(y_dram, bass.IndirectOffsetOnAxis(ap=to_i[:], axis=0), y_sb[:], None).then_inc(y_sent, 16)

                pool.wait_ge(first_set, 1)
                scatter()

                def tile(i, e, q, s, lo):
                    pool.wait_ge(y_ready, s + 2)
                    pool.sem_inc(pool_steps, 1)
                    scatter()
                experts(pool, nothing, tile, nothing)
                tiles = pool.value_load(tiles_i[0:1, EX:EX + 1], min_val=EX, max_val=MAXT)
                pool.wait_ge(y_sent, tiles * 16 + 16)

            @block.scalar
            def _(act):
                act.sem_inc(hT_ready, 1)
                for q in range(2):
                    load_expert(act, q, q)

                def tile(i, e, q, s, lo):
                    act.wait_ge(down_done, s + 1)
                    for f in range(FB):
                        act.wait_ge(up_done, s * FB + (f + 1))
                        act.activation(hT[:, f, :], bk[f][:, 0:P], ACT.Relu,
                                       bias=b1_cols[:, ds(e * FB + f, 1)]).then_inc(hT_ready, 1)

                def end(i, e, q, hi):
                    act.wait_ge(down_done, hi + 1)
                    act.sem_inc(sp_steps, 1)
                    with act.If(i < EX // 2 - 1):
                        load_expert(act, (e + 2).with_bounds(min_val=2, max_val=EX - 1), q)
                    act.nop()
                experts(act, nothing, tile, end)

            @block.tensor
            def _(pe):
                def turn_tile():
                    for b in range(NB):
                        s = nc.tensor.transpose(bk[4][:, b * P:(b + 1) * P], xt[:, b * P:(b + 1) * P], ident[:])
                    s.then_inc(xt_turned, 1)

                pe.sem_inc(down_done, 1)
                pe.sem_inc(xt_turned, 1)
                pe.wait_ge(xt_in, 16)
                turn_tile()

                def start(i, e, q):
                    pe.wait_ge(w1_in[q], i * 32 + 32)
                    pe.sem_inc(pe_steps, 1)

                def tile(i, e, q, s, lo):
                    pe.wait_ge(xtT_ready, s + 1)
                    pe.wait_ge(hT_ready, s * FB + 1)
                    for f in range(FB):
                        for b in range(NB):
                            m = nc.tensor.matmul(bk[f][:, 0:P], w1_sb[:, q, b, f * P:(f + 1) * P], xtT[:, b, :],
                                                 start=b == 0, stop=b == NB - 1)
                        m.then_inc(up_done, 1)
                    pe.wait_ge(xt_in, s * 16 + 32)
                    turn_tile()
                    pe.wait_ge(y_ready, s + 1)
                    for f in range(FB):
                        pe.wait_ge(hT_ready, s * FB + (f + 2))
                        m = nc.tensor.matmul(bk[5][:, 0:D], hT[:, f, :], w2_sb[:, q, f, :], start=f == 0, stop=f == FB - 1)
                    m.then_inc(down_done, 1)
                experts(pe, start, tile, nothing)

            @block.vector
            def _(dve):
                link = Chain(dve, expert_own)
                v = nc.vector

                def take_tile():
                    v.tensor_copy(held[:], xt[:, TOKEN:CHOICE + 1]).then_inc(xt_read, 1)
                    v.tensor_copy(xtT[:], bk[4][:, 0:D].rearrange("p (b n) -> p b n", b=NB)).then_inc(xtT_ready, 1)

                dve.sem_inc(xt_read, 1)
                dve.sem_inc(y_ready, 1)
                v.memset(y_sb[:], 0.0)
                v.tensor_scalar(to_i[:], part_f[:], float(2 * NP), None, ALU.add).then_inc(first_set, 1)
                dve.wait_ge(xt_turned, 2)
                take_tile()
                held_steps = 1

                def tile(i, e, q, s, lo):
                    dve.wait_ge(xt_read, s + 2)
                    v.tensor_scalar(other[:], held[:, 1:2], iota_f[:, ds(e, 1)], float(NP), ALU.not_equal, ALU.mult).then_inc(expert_own, 1)
                    dve.wait_ge(expert_own, s * 2 + 1)
                    dve.wait_ge(y_sent, s * 16 + 16)
                    v.tensor_tensor(to_i[:], other[:], held[:, 0:1], ALU.add).then_inc(expert_own, 1)
                    dve.wait_ge(expert_own, s * 2 + 2)
                    dve.wait_ge(xt_turned, s + 3)
                    dve.wait_ge(up_done, s * FB + FB)
                    take_tile()
                    dve.wait_ge(down_done, s + 2)
                    v.tensor_tensor(y_sb[:], bk[5][:, 0:D], b2_b[:, ds(e, 1), :].rearrange("p e d -> p (e d)"), ALU.add).then_inc(y_ready, 1)
                experts(dve, nothing, tile, nothing)
        expert_stage.close()

        last_stage = ctx.enter_context(ExitStack())

        def sb(name, shape, dt):
            return last_stage.enter_context(nc.sbuf_tensor(name, shape, dt))

        ya = [sb(f"ya{q}", [P, WB, D], fp32) for q in range(2)]
        yb = [sb(f"yb{q}", [P, WB, D], fp32) for q in range(2)]
        xn2 = [sb(f"xn2_{q}", [P, WB, D], fp32) for q in range(2)]
        stats3 = sb("stats3", [P, WB, 6], fp32)
        mv3 = sb("mv3", [P, WB, 2], fp32)
        std3 = sb("std3", [P, WB], fp32)
        rs3 = sb("rs3", [P, WB], fp32)
        sh3 = sb("sh3", [P, WB], fp32)

        y_in = [sem(f"y_in{q}") for q in range(2)]
        xn2_ready = sem("xn2_ready")
        mv3_ready = sem("mv3_ready")
        std3_ready = sem("std3_ready")
        norm3_ready = sem("norm3_ready")
        yn_ready = sem("yn_ready")
        scaled = sem("scaled")
        out_ready = sem("out_ready")
        out_sent = [sem(f"out_sent{q}") for q in range(2)]
        last_own = sem("last_own")

        with nc.Block() as block:
            @block.sync
            def _(sp):
                def load(t, q):
                    if q == 0:
                        await_turn(sp, out_sent[0], t, 8, 0)
                    else:
                        await_turn(sp, out_sent[1], t, 8, -8)
                    for k, to in enumerate((ya[q], yb[q])):
                        sp.dma_start(to[:], y_dram[ds(t * (WB * P) + k * NP, WB * P), :].rearrange("(w p) d -> p w d", p=P)).then_inc(y_in[q], 16)

                def store(t, q):
                    sp.wait_ge(out_ready, t + 1)
                    sp.dma_start(out[ds(t * (WB * P), WB * P), :].rearrange("(w p) d -> p w d", p=P), ya[q][:]).then_inc(out_sent[q], 16)

                load(0, 0)
                with sp.Fori(0, (WT - 1) // 2) as i:
                    load(i * 2 + 1, 1)
                    store(i * 2, 0)
                    load(i * 2 + 2, 0)
                    store(i * 2 + 1, 1)
                sp.wait_ge(out_ready, WT)
                w0 = (WT - 1) * WB
                sp.dma_start(out[w0 * P:(NW - 1) * P, :].rearrange("(w p) d -> p w d", p=P), ya[0][:, 0:WB - 1, :]).then_inc(out_sent[0], 16)
                sp.dma_start(out[(NW - 1) * P:N, :], ya[0][0:LASTW, WB - 1, :]).then_inc(out_sent[0], 16)
                sp.wait_ge(out_sent[0], 16 * ((WT - 1) // 2 + 2))
                sp.wait_ge(out_sent[1], 16 * (WT // 2))

            @block.scalar
            def _(act):
                def norm_input(t, q):
                    await_turn(act, scaled, t, 1, -1)
                    for j in range(WB):
                        act.activation(xn2[q][:, j, :], x1[:, ds(t * WB + j, 1), :].rearrange("p w d -> p (w d)"), ACT.Identity,
                                       bias=shift2[:, ds(t * WB + j, 1)], scale=rstd2[:, ds(t * WB + j, 1)]).then_inc(xn2_ready, 1)

                def body(t, q):
                    norm_input(t, q)
                    act.wait_ge(mv3_ready, t + 1)
                    act.activation(std3[:], mv3[:, :, 1], ACT.Sqrt, bias=eps[:]).then_inc(std3_ready, 1)
                    act.wait_ge(norm3_ready, t + 1)
                    for j in range(WB):
                        s = act.activation(xn2[q][:, j, :], yb[q][:, j, :], ACT.Identity, bias=sh3[:, j:j + 1], scale=rs3[:, j:j + 1])
                    s.then_inc(yn_ready, 1)
                window_turns(act, body)

            @block.gpsimd
            def _(pool):
                def body(t, q):
                    pool.wait_ge(yn_ready, t + 1)
                    pool.tensor_tensor(xn2[q][:], xn2[q][:], gamma_b[:, None, :].to_broadcast([P, WB, D]), ALU.mult).then_inc(scaled, 1)
                window_turns(pool, body)

            @block.vector
            def _(dve):
                link = Chain(dve, last_own)
                v = nc.vector

                def body(t, q):
                    link.enter(t, 5)
                    dve.wait_ge(y_in[q], (t + (2 - q)) * 16)
                    here = x1[:, ds(t * WB, WB), :]
                    for j in range(WB):
                        dve.wait_ge(xn2_ready, t * WB + (j + 1))
                        s = v.scalar_tensor_tensor(ya[q][:, j, :], ya[q][:, j, :], first_w[:, ds(t * WB + j, 1)], xn2[q][:, j, :], ALU.mult, ALU.add)
                    link(s)
                    for j in range(WB):
                        s = v.scalar_tensor_tensor(yb[q][:, j, :], yb[q][:, j, :], second_w[:, ds(t * WB + j, 1)], ya[q][:, j, :], ALU.mult, ALU.add)
                    link(s)
                    for j in range(WB):
                        s = v.bn_stats(stats3[:, j, :], yb[q][:, j, :])
                    link(s)
                    dve.sem_inc(dve_steps, 1)
                    for j in range(WB):
                        s = v.bn_aggr(mv3[:, j, :], stats3[:, j, :])
                    s.then_inc(mv3_ready, 1)
                    v.tensor_tensor(here, here, beta_b[:, None, :].to_broadcast([P, WB, D]), ALU.add)
                    dve.wait_ge(std3_ready, t + 1)
                    link(v.reciprocal(rs3[:], std3[:]))
                    link(v.scalar_tensor_tensor(sh3[:], mv3[:, :, 0], -1.0, rs3[:], ALU.mult, ALU.mult))
                    dve.sem_inc(norm3_ready, 1)
                    dve.wait_ge(scaled, t + 1)
                    v.tensor_tensor(ya[q][:], xn2[q][:], here, ALU.add).then_inc(out_ready, 1)
                window_turns(dve, body)
                link.leave(WT)
        last_stage.close()


_INS = ['x', 'src', 'dst', 'edge_weight', 'L0_gnn_W', 'L0_ffn_gate_w', 'L0_ffn_gate_b', 'L0_ffn_w1', 'L0_ffn_b1',
        'L0_ffn_w2', 'L0_ffn_b2', 'L0_ffn_gamma', 'L0_ffn_beta']
_OUTS = [((6250, 256), 'float32')]


def kernel(**inputs):
    import numpy as _np
    import concourse.bacc as _bacc
    from concourse import mybir as _mybir
    from concourse.bass_utils import run_bass_kernel_spmd as _run

    nc = _bacc.Bacc("TRN2", target_bir_lowering=False, num_devices=1)
    arrays, args = {}, []
    for name in _INS:
        a = _np.ascontiguousarray(inputs[name])
        arrays[f"in_{name}_dram"] = a
        args.append(nc.dram_tensor(f"in_{name}_dram", a.shape, _mybir.dt.from_np(a.dtype), kind="ExternalInput").ap())
    for i, (shape, dtype) in enumerate(_OUTS):
        dt = _mybir.dt.from_np(_np.dtype(dtype))
        args.append(nc.dram_tensor(f"out_{i}_dram", shape, dt, kind="ExternalOutput").ap())
    gnn_moe_kernel(nc, *args)
    r = _run(nc, [arrays], core_ids=[0])
    got = tuple(r.results[0][f"out_{i}_dram"] for i in range(len(_OUTS)))
    return got[0]
```

```python
import concourse.bass as bass
from concourse import mybir
from contextlib import ExitStack


class Chain:

    def __init__(self, engine, done):
        self.engine, self.done, self.base, self.n, self.per, self.turn = engine, done, 0, 0, 0, 0

    def enter(self, turn, per):
        if not self.per:
            self.base += self.n
        self.turn, self.per, self.n = turn, per, 0

    def leave(self, turns):
        assert self.n == self.per, (self.n, self.per)
        self.base, self.per, self.turn, self.n = self.base + turns * self.per, 0, 0, 0

    def __call__(self, instruction):
        instruction.then_inc(self.done, 1)
        self.n += 1
        self.engine.wait_ge(self.done, self.turn * self.per + (self.base + self.n))


def await_turn(engine, sem, turn, per, value):
    if isinstance(turn, int):
        if per * turn + value > 0:
            engine.wait_ge(sem, per * turn + value)
    else:
        engine.wait_ge(sem, turn * per + value)


def gnn_moe_kernel(nc, x, src, dst, edge_weight, gnn_w, gate_w, gate_b, w1, b1, w2, b2, gamma, beta, out):
    fp32, bf16, i32, u32 = mybir.dt.float32, mybir.dt.bfloat16, mybir.dt.int32, mybir.dt.uint32
    ALU, ACT, AX = mybir.AluOpType, mybir.ActivationFunctionType, mybir.AxisListType
    ds = bass.ds

    P = 128
    N, D = x.shape
    NE = src.shape[0]
    EX, _, F = w1.shape
    EPS = 1e-5
    NB = D // P
    NW = -(-N // P)
    WB = 7
    WT = NW // WB
    assert WB * WT == NW
    NP = NW * P
    LASTW = N - (NW - 1) * P
    GT = 8
    GE = GT * P
    NG = -(-NE // GE)
    NG += NG % 2
    FULL = NE // GE
    REST = NE - FULL * GE
    COPIES = 4
    JUNK = NP
    ROWS = NP + P
    GB = 2
    GTURNS = NG // GB
    PAIRS = GT // 2
    PT = GB * PAIRS
    LAG = 3

    FB = F // P
    CAP = NP + P
    RW = 264
    TOKEN, CHOICE = D, D + 1
    slots_dram = nc.dram_tensor("slots", [EX * CAP, RW], fp32).ap()
    y_dram = nc.dram_tensor("expert_out", [2 * NP + 5 * P, D], fp32).ap()
    h_rows_dram = nc.dram_tensor("h_rows", [NP, D], fp32).ap()
    src_dram = nc.dram_tensor("src_padded", [NG, GE], i32).ap()
    table_dram = nc.dram_tensor("group_table", [NG, 2], fp32).ap()
    acc = [nc.dram_tensor(f"acc{c}", [ROWS, D], fp32).ap() for c in range(COPIES)]

    ctx = ExitStack()
    with ctx:
        def sb(name, shape, dt):
            return ctx.enter_context(nc.sbuf_tensor(name, shape, dt))

        def bank(name, shape, dt=fp32):
            return ctx.enter_context(nc.psum_tensor(name, shape, dt))

        def sem(name):
            return ctx.enter_context(nc.semaphore(name))

        ones = sb("ones", [P, P], fp32)
        ident = sb("ident", [P, P], fp32)
        iota_i = sb("iota_i", [P, P], i32)
        iota_f = sb("iota_f", [P, P], fp32)
        part_i = sb("part_i", [P, 1], i32)
        part_f = sb("part_f", [P, 1], fp32)
        junk_row = sb("junk_row", [P, 1], fp32)
        before = sb("before", [P, P], fp32)
        eps = sb("eps", [P, 1], fp32)

        x1 = sb("x1", [P, NW, D], fp32)
        rstd2 = sb("rstd2", [P, NW], fp32)
        shift2 = sb("shift2", [P, NW], fp32)
        top2 = sb("top2", [P, NW, 2], fp32)
        first_w = sb("first_w", [P, NW], fp32)
        second_w = sb("second_w", [P, NW], fp32)
        upper = sb("upper", [P, P], bf16)
        ones_b = sb("ones_b", [P, P], bf16)
        gate_sb = sb("gate_sb", [P, NB, EX], fp32)
        gate_bb = sb("gate_bb", [P, EX], fp32)
        expert_base = sb("expert_base", [P, EX], fp32)
        carry = sb("carry", [P, EX], bf16)
        carry_f = sb("carry_f", [P, EX], fp32)
        filler = sb("filler", [P, 2, RW], fp32)
        tok = sb("tok", [P, WB], fp32)
        counts_f = sb("counts_f", [1, EX], fp32)
        counts_i = sb("counts_i", [1, EX], i32)
        ntiles_i = sb("ntiles_i", [1, EX], i32)
        ntiles_f = sb("ntiles_f", [1, EX], fp32)
        ends_f = sb("ends_f", [1, EX], fp32)
        tiles_i = sb("tiles_i", [1, EX + 1], i32)
        w1_sb = sb("w1_sb", [P, 2, NB, F], fp32)
        w2_sb = sb("w2_sb", [P, 2, FB, D], fp32)
        b1_rows = sb("b1_rows", [EX * FB, P], fp32)
        b1_cols = sb("b1_cols", [P, EX * FB], fp32)
        b2_b = sb("b2_b", [P, EX, D], fp32)
        gamma_b = sb("gamma_b", [P, D], fp32)
        beta_b = sb("beta_b", [P, D], fp32)

        layer1 = ctx.enter_context(ExitStack())

        def sb(name, shape, dt):
            return layer1.enter_context(nc.sbuf_tensor(name, shape, dt))

        table_b = sb("table_b", [P, NG, 2], fp32)
        table_i = sb("table_i", [1, NG * 2], i32)
        gathers_i = sb("gathers_i", [1, NG], i32)
        SRC, WGT, REL, OFF, DST = range(5)
        cols = sb("cols", [P, NG, 5, GT], fp32)

        prepare = ctx.enter_context(ExitStack())

        def sb(name, shape, dt):
            return prepare.enter_context(nc.sbuf_tensor(name, shape, dt))

        stats = sb("stats", [P, NW, 6], fp32)
        mv = sb("mv", [P, NW, 2], fp32)
        zeros = sb("zeros", [P, 10 * D], fp32)
        upper_f = sb("upper_f", [P, P], fp32)
        std = sb("std", [P, NW], fp32)
        rstd = sb("rstd", [P, NW], fp32)
        shift = sb("shift", [P, NW], fp32)
        xn = sb("xn", [P, WB, D], fp32)
        xnT = sb("xnT", [P, WB, NB, P], fp32)
        w_rows = sb("w_rows", [P, NB, D], fp32)
        wT = sb("wT", [P, NB, D], fp32)
        src_rows = sb("src_rows", [NG, GE], i32)
        dst_rows = sb("dst_rows", [NG, GE], i32)
        wgt_rows = sb("wgt_rows", [NG, GE], fp32)
        src_rf = sb("src_rf", [NG, GE], fp32)
        dst_rf = sb("dst_rf", [NG, GE], fp32)
        lohi = sb("lohi", [NG, 2], fp32)
        span = sb("span", [NG, 1], fp32)
        table = sb("table", [NG, 2], fp32)
        slow_f = sb("slow_f", [1, NG], fp32)
        slows_f = sb("slows_f", [1, NG], fp32)

        bk = [bank(f"bank{i}", [P, 512]) for i in range(8)]

        x_in = sem("x_in")
        x_read = sem("x_read")
        b1_taken = sem("b1_taken")
        w_in = sem("w_in")
        pads_set = sem("pads_set")
        edges_in = sem("edges_in")
        consts = sem("consts")
        zero_set = sem("zero_set")
        acc_init = sem("acc_init")
        pool_own = sem("pool_own")
        dve_own = sem("dve_own")
        dve_step = sem("dve_step")
        pool_steps = sem("pool_steps")
        dve_steps = sem("dve_steps")
        act_steps = sem("act_steps")
        pe_steps = sem("pe_steps")
        sp_steps = sem("sp_steps")
        later_in = sem("later_in")
        b1_in = sem("b1_in")
        b1_turned = sem("b1_turned")
        w_t = sem("w_t")
        wT_ready = sem("wT_ready")
        mv_ready = sem("mv_ready")
        std_ready = sem("std_ready")
        shift_ready = sem("shift_ready")
        xn_ready = sem("xn_ready")
        xn_turned = sem("xn_turned")
        xnT_ready = sem("xnT_ready")
        h_done = sem("h_done")
        h_copied = sem("h_copied")
        h_stored = sem("h_stored")
        src_stored = sem("src_stored")
        table_ready = sem("table_ready")
        table_stored = sem("table_stored")
        table_back = sem("table_back")
        floats_ready = sem("floats_ready")
        cols_turned = sem("cols_turned")
        cols_taken = sem("cols_taken")
        src_b_in = [sem(f"src_b_in{q}") for q in range(GB)]
        h_in = [sem(f"h_in{q}") for q in range(GB)]
        gathered = sem("gathered")
        rows_ready = sem("rows_ready")
        dst_ready = sem("dst_ready")
        pick_ready = sem("pick_ready")
        mixed = sem("mixed")
        mix_ready = sem("mix_ready")
        summed = sem("summed")
        msg_ready = sem("msg_ready")
        added = [sem(f"added{c}") for c in range(COPIES)]
        w_expert_in = [sem(f"w_expert_in{q}") for q in range(2)]

        def turn_loop(engine, body):
            body(0)
            with engine.Fori(1, WT) as t:
                body(t)

        RING = 4
        A = ROWS // P
        ZA = zeros.shape[1] // D

        def earlier(j):
            return j - RING + 1 if j >= RING else (j + RING if j + RING < WB else j) - WB + 1

        with nc.Block() as block:
            @block.sync
            def _(sp):
                sp.wait_ge(pads_set, 3)
                for rows, given in ((src_rows, src), (dst_rows, dst), (wgt_rows, edge_weight)):
                    sp.dma_start(rows[0:FULL, :], given[0:FULL * GE].rearrange("(g e) -> g e", e=GE)).then_inc(edges_in, 16)
                    sp.dma_start(rows[FULL:FULL + 1, 0:REST], given[FULL * GE:NE].rearrange("(g e) -> g e", g=1)).then_inc(edges_in, 16)
                sp.dma_start(w_rows[:], gnn_w.rearrange("(b p) d -> p b d", p=P)).then_inc(w_in, 16)
                sp.dma_start(b1_rows[:], b1.rearrange("e (b p) -> (e b) p", p=P)).then_inc(b1_in, 16)
                for t in range(WT - 1):
                    sp.dma_start(x1[:, t * WB:(t + 1) * WB, :],
                                 x[t * WB * P:(t + 1) * WB * P, :].rearrange("(w p) d -> p w d", p=P)).then_inc(x_in, 16)
                sp.wait_ge(pads_set, 4)
                w0 = (WT - 1) * WB
                sp.dma_start(x1[:, w0:NW - 1, :],
                             x[w0 * P:(NW - 1) * P, :].rearrange("(w p) d -> p w d", p=P)).then_inc(x_in, 16)
                sp.dma_start(x1[0:LASTW, NW - 1, :], x[(NW - 1) * P:N, :]).then_inc(x_in, 16)
                sp.wait_ge(edges_in, 96)
                sp.dma_start(src_dram, src_rows[:]).then_inc(src_stored, 16)
                sp.wait_ge(table_ready, 1)
                sp.dma_start(table_dram, table[:]).then_inc(table_stored, 16)
                sp.wait_ge(table_stored, 16)
                sp.dma_start(table_b[:], table_dram.partition_broadcast(P)).then_inc(table_back, 16)
                sp.dma_start(acc[0][0:(NW - 1) * P, :].rearrange("(p a) d -> p (a d)", p=P),
                             x[0:(NW - 1) * P, :].rearrange("(p a) d -> p (a d)", p=P)).then_inc(acc_init, 16)
                sp.dma_start(acc[0][(NW - 1) * P:N, :], x[(NW - 1) * P:N, :]).then_inc(acc_init, 16)
                sp.wait_ge(zero_set, 1)
                sp.dma_start(acc[0][N:NP, :], zeros[0:NP - N, 0:D]).then_inc(acc_init, 16)
                sp.dma_start(acc[0][NP:ROWS, :], zeros[:, 0:D]).then_inc(acc_init, 16)
                for c in range(1, COPIES):
                    rows = acc[c].rearrange("(p a) d -> p (a d)", p=P)
                    for a in range(0, A, ZA):
                        sp.dma_start(rows[:, a * D:(a + ZA) * D], zeros[:]).then_inc(acc_init, 16)
                sp.dma_start(gate_sb[:], gate_w.rearrange("(b p) e -> p b e", p=P)).then_inc(later_in, 16)
                for to, given in ((gate_bb, gate_b), (b2_b, b2), (gamma_b, gamma), (beta_b, beta)):
                    sp.dma_start(to[:], given.partition_broadcast(P)).then_inc(later_in, 16)

                def body(t):
                    sp.wait_ge(h_copied, t * WB + WB)
                    sp.dma_start(h_rows_dram[ds(t * (WB * P), WB * P), :].rearrange("(w p) d -> p w d", p=P),
                                 x1[:, ds(t * WB, WB), :]).then_inc(h_stored, 16)
                turn_loop(sp, body)
                sp.wait_ge(h_stored, 16 * WT)
                sp.wait_ge(src_stored, 16)
                sp.wait_ge(later_in, 16 * 5)
                sp.wait_ge(acc_init, 16 * (4 + (COPIES - 1) * A // ZA))

            @block.gpsimd
            def _(pool):
                link = Chain(pool, pool_own)
                pool.memset(src_rows[:], 0).then_inc(pads_set, 1)
                pool.memset(dst_rows[:], N - 1).then_inc(pads_set, 1)
                pool.memset(wgt_rows[:], 0.0).then_inc(pads_set, 1)
                pool.memset(x1[:, NW - 1, :], 0.0).then_inc(pads_set, 1)
                link(pool.memset(ident[:], 0.0))
                pool.affine_select(out=ident[:], in_=ident[:], compare_op=ALU.not_equal, fill=1.0, base=0,
                                   pattern=[[-1, P]], channel_multiplier=1).then_inc(consts, 1)
                link(pool.memset(ones[:], 1.0))
                pool.affine_select(out=before[:], in_=ones[:], compare_op=ALU.is_gt, fill=0.0, base=0,
                                   pattern=[[-1, P]], channel_multiplier=1).then_inc(consts, 1)
                pool.memset(ones_b[:], 1.0).then_inc(consts, 1)
                pool.affine_select(out=upper_f[:], in_=ones[:], compare_op=ALU.is_gt, fill=0.0, base=0,
                                   pattern=[[1, P]], channel_multiplier=-1).then_inc(consts, 1)
                pool.iota(iota_i[:], [[1, P]], base=0, channel_multiplier=0).then_inc(consts, 1)
                pool.iota(part_i[:], [[0, 1]], base=0, channel_multiplier=1).then_inc(consts, 1)
                pool.memset(eps[:], EPS).then_inc(consts, 1)
                pool.memset(zeros[:], 0.0).then_inc(zero_set, 1)

            @block.scalar
            def _(act):
                def copy_h(t, j):
                    act.wait_ge(h_done, t * WB + (j + 1))
                    act.sem_inc(act_steps, 1)
                    act.activation(x1[:, ds(t * WB + j, 1), :].rearrange("p w d -> p (w d)"), bk[4 + j % RING][:, 0:D],
                                   ACT.Copy).then_inc(h_copied, 1)

                act.wait_ge(mv_ready, 1)
                act.activation(std[:], mv[:, :, 1], ACT.Sqrt, bias=eps[:]).then_inc(std_ready, 1)
                act.wait_ge(shift_ready, 1)

                def body(t):
                    for j in range(WB):
                        await_turn(act, xn_turned, t, WB, j + 1 - WB)
                        act.activation(xn[:, j, :], x1[:, ds(t * WB + j, 1), :].rearrange("p w d -> p (w d)"), ACT.Identity,
                                       bias=shift[:, ds(t * WB + j, 1)], scale=rstd[:, ds(t * WB + j, 1)]).then_inc(xn_ready, 1)
                        if j >= LAG:
                            copy_h(t, j - LAG)
                        elif not isinstance(t, int):
                            copy_h(t - 1, j - LAG + WB)
                turn_loop(act, body)
                for j in range(WB - LAG, WB):
                    copy_h(WT - 1, j)

            @block.vector
            def _(dve):
                link = Chain(dve, dve_own)
                v = nc.vector
                dve.wait_ge(consts, 7)
                link(v.tensor_copy(iota_f[:], iota_i[:]))
                v.tensor_copy(upper[:], upper_f[:])
                link(v.tensor_copy(part_f[:], part_i[:]))
                link(v.tensor_scalar(junk_row[:], part_f[:], float(JUNK), None, ALU.add))
                dve.wait_ge(edges_in, 96)
                v.tensor_copy(dst_rf[:], dst_rows[:]).then_inc(floats_ready, 1)
                v.tensor_copy(src_rf[:], src_rows[:]).then_inc(floats_ready, 1)
                dve.wait_ge(floats_ready, 1)
                v.tensor_reduce(lohi[:, 0:1], dst_rf[:], AX.X, ALU.min)
                link(v.tensor_reduce(lohi[:, 1:2], dst_rf[:], AX.X, ALU.max))
                link(v.tensor_scalar(table[:, 0:1], lohi[:, 0:1], float(NP - P), None, ALU.min))
                link(v.tensor_tensor(span[:], lohi[:, 1:2], table[:, 0:1], ALU.subtract))
                v.tensor_scalar(table[:, 1:2], span[:], float(P - 1), None, ALU.is_gt).then_inc(table_ready, 1)
                for n, field in enumerate((DST, SRC, WGT)):
                    for half in range(2):
                        dve.wait_ge(cols_turned, 2 * n + half + 1)
                        v.tensor_copy(cols[:, :, field, 4 * half:4 * half + 4],
                                      bk[6 + half][:, 0:4 * NG].rearrange("p (j g) -> p g j", j=4)).then_inc(cols_taken, 1)
                for b in range(NB):
                    dve.wait_ge(w_t, b + 1)
                    v.tensor_copy(wT[:, b, :], bk[b][:, 0:D]).then_inc(wT_ready, 1)
                dve.wait_ge(b1_turned, 1)
                v.tensor_copy(b1_cols[:], bk[2][:, 0:EX * FB]).then_inc(b1_taken, 1)
                dve.wait_ge(x_in, 16 * (WT + 1))
                with dve.Fori(0, WT) as t:
                    for j in range(WB):
                        s = v.bn_stats(stats[:, ds(t * WB + j, 1), :].rearrange("p w s -> p (w s)"),
                                       x1[:, ds(t * WB + j, 1), :].rearrange("p w d -> p (w d)"))
                    s.then_inc(x_read, 1)
                dve.wait_ge(x_read, WT)
                for w in range(NW):
                    s = v.bn_aggr(mv[:, w, :], stats[:, w, :])
                s.then_inc(mv_ready, 1)
                dve.wait_ge(std_ready, 1)
                link(v.reciprocal(rstd[:], std[:]))
                v.scalar_tensor_tensor(shift[:], mv[:, :, 0], -1.0, rstd[:], ALU.mult, ALU.mult).then_inc(shift_ready, 1)

                def body(t):
                    for j in range(WB):
                        dve.wait_ge(xn_turned, t * WB + (j + 1))
                        await_turn(dve, h_done, t, WB, j + 1 - WB)
                        v.tensor_copy(xnT[:, j, :, :], bk[j % RING][:, 0:D].rearrange("p (b n) -> p b n", b=NB)).then_inc(xnT_ready, 1)
                turn_loop(dve, body)
                dve.wait_ge(cols_taken, 6)
                dve.wait_ge(table_back, 16)
                lo = table_b[:, :, 0:1].to_broadcast([P, NG, GT])
                slow = table_b[:, :, 1:2].to_broadcast([P, NG, GT])
                rel, off = cols[:, :, REL, :], cols[:, :, OFF, :]
                v.tensor_scalar(off, cols[:, :, SRC, :], junk_row[:], None, ALU.subtract)
                v.tensor_copy(table_i[:], table_b[0:1, :, :].rearrange("p g c -> p (g c)"))
                link(v.tensor_copy(slow_f[:], table_b[0:1, :, 1:2].rearrange("p g c -> p (g c)")))
                link(v.tensor_tensor_scan(slows_f[:], ones[0:1, 0:NG], slow_f[:], 0.0, ALU.mult, ALU.add))
                v.tensor_scalar(gathers_i[:], slows_f[:], 16.0 * GT, None, ALU.mult)
                link(v.tensor_tensor(rel, cols[:, :, DST, :], lo, ALU.subtract))
                link(v.tensor_scalar(rel, rel, part_f[:], None, ALU.subtract))
                link(v.tensor_scalar(table_b[:, :, 1:2], table_b[:, :, 1:2], -1.0, 1.0, ALU.mult, ALU.add))
                link(v.tensor_tensor(rel, rel, slow, ALU.mult))
                link(v.tensor_scalar(rel, rel, part_f[:], None, ALU.add))

            @block.tensor
            def _(pe):
                pe.wait_ge(consts, 7)
                for n, rows in enumerate((dst_rf, src_rf, wgt_rows)):
                    pe.wait_ge(floats_ready, min(n + 1, 2))
                    for half in range(2):
                        if n > 0:
                            pe.wait_ge(cols_taken, 2 * n + half - 1)
                        for j in range(4):
                            e = (4 * half + j) * P
                            s = nc.tensor.transpose(bk[6 + half][:, j * NG:(j + 1) * NG], rows[:, e:e + P], ident[0:NG, 0:NG])
                        s.then_inc(cols_turned, 1)
                pe.wait_ge(w_in, 16)
                for b in range(NB):
                    for a in range(NB):
                        s = nc.tensor.transpose(bk[b][:, a * P:(a + 1) * P], w_rows[:, a, b * P:(b + 1) * P], ident[:])
                    s.then_inc(w_t, 1)
                pe.wait_ge(b1_in, 16)
                nc.tensor.transpose(bk[2][:, 0:EX * FB], b1_rows[:], ident[0:EX * FB, 0:EX * FB]).then_inc(b1_turned, 1)
                pe.wait_ge(wT_ready, NB)
                pe.wait_ge(b1_taken, 1)
                pe.wait_ge(cols_taken, 6)

                def product(t, j):
                    pe.wait_ge(xnT_ready, t * WB + (j + 1))
                    await_turn(pe, h_copied, t, WB, earlier(j))
                    for b in range(NB):
                        s = nc.tensor.matmul(bk[4 + j % RING][:, 0:D], xnT[:, j, b, :], wT[:, b, :],
                                             start=b == 0, stop=b == NB - 1)
                    s.then_inc(h_done, 1)

                def body(t):
                    for j in range(WB):
                        pe.wait_ge(xn_ready, t * WB + (j + 1))
                        await_turn(pe, xnT_ready, t, WB, earlier(j))
                        for b in range(NB):
                            s = nc.tensor.transpose(bk[j % RING][:, b * P:(b + 1) * P], xn[:, j, b * P:(b + 1) * P], ident[:])
                        s.then_inc(xn_turned, 1)
                        if j > 0:
                            product(t, j - 1)
                        elif not isinstance(t, int):
                            product(t - 1, WB - 1)
                turn_loop(pe, body)
                product(WT - 1, WB - 1)
        prepare.close()

        def sb(name, shape, dt):
            return layer1.enter_context(nc.sbuf_tensor(name, shape, dt))

        cols_s = sb("cols_s", [P, GB, 5, GT], fp32)
        src_b = sb("src_b", [P, GB, GE], i32)
        h_buf = sb("h_buf", [P, GB, GT, D], fp32)
        dup = sb("dup", [P, GB, GT], fp32)
        row_f = sb("row_f", [P, GB, GT], fp32)
        row_i = sb("row_i", [P, GB, GT], i32)
        dst_i = sb("dst_i", [P, GB, GT], i32)
        merge = sb("merge", [P, GB, GT, P], fp32)
        pick = sb("pick", [P, GB, GT, P], fp32)
        mix = sb("mix", [P, 2, 2, P], fp32)
        msg = sb("msg", [P, 4, 2, D], fp32)

        def turns(engine, body):
            body(0)
            with engine.Fori(1, GTURNS) as i:
                body(i)

        def load_expert(engine, e, q):
            engine.dma_start(w1_sb[:, q, :, :], w1[ds(e, 1), :, :].rearrange("e (b p) f -> p (e b) f", p=P)).then_inc(w_expert_in[q], 16)
            engine.dma_start(w2_sb[:, q, :, :], w2[ds(e, 1), :, :].rearrange("e (b p) d -> p (e b) d", p=P)).then_inc(w_expert_in[q], 16)

        with nc.Block() as block:
            @block.sync
            def _(sp):
                def body(i):
                    for q in range(GB):
                        await_turn(sp, pick_ready, i, GB * GT, GT * (q + 1) - GB * GT)
                        sp.dma_start(src_b[:, q, :], src_dram[ds(i * GB + q, 1), :].to_broadcast([P, GE])).then_inc(src_b_in[q], 16)
                        slow = sp.value_load(table_i[0:1, ds(i * (2 * GB) + (2 * q + 1), 1)], min_val=0, max_val=1)
                        lo = sp.value_load(table_i[0:1, ds(i * (2 * GB) + 2 * q, 1)], min_val=0, max_val=NP - P)
                        await_turn(sp, summed, i, PT, PAIRS * (q + 1) - PT)
                        sp.sem_inc(sp_steps, 1)
                        with sp.If(slow == 0):
                            sp.dma_start(h_buf[:, q, 0, :], h_rows_dram[ds(lo, P), :]).then_inc(h_in[q], 16)
                        sp.nop()
                for q in range(2):
                    load_expert(sp, q, q)
                turns(sp, body)

            @block.gpsimd
            def _(pool):
                def settled():
                    pool.sem_inc(pool_steps, 1)

                def body(i):
                    for q in range(GB):
                        pool.wait_ge(dst_ready, i * GB + (q + 1))
                        slow = pool.value_load(table_i[0:1, ds(i * (2 * GB) + (2 * q + 1), 1)], min_val=0, max_val=1)
                        with pool.If(slow == 1):
                            await_turn(pool, summed, i, PT, PAIRS * (q + 1) - PT)
                            settled()
                            for j in range(GT):
                                pool.indirect_dma_start(h_buf[:, q, j, :], None, h_rows_dram,
                                                        bass.IndirectOffsetOnAxis(ap=dst_i[:, q, j:j + 1], axis=0)).then_inc(gathered, 16)
                            pool.wait_ge(gathered, pool.value_load(gathers_i[0:1, ds(i * GB + q, 1)], min_val=16 * GT, max_val=16 * GT * NG))
                            pool.sem_inc(h_in[q], 16)
                        pool.wait_ge(rows_ready, i * GB + (q + 1))
                        for j in range(GT):
                            u = q * GT + j
                            c = u % COPIES
                            if j % 2 == 0:
                                pool.wait_ge(msg_ready, i * PT + (u // 2 + 1))
                            per = 16 * GB * GT // COPIES
                            await_turn(pool, added[c], i, per, 16 * (u // COPIES))
                            settled()
                            pool.indirect_dma_start(acc[c], bass.IndirectOffsetOnAxis(ap=row_i[:, q, j:j + 1], axis=0),
                                                    msg[:, (u // 2) % 4, j % 2, :], None,
                                                    compute_op=ALU.add).then_inc(added[c], 16)
                turns(pool, body)
                for c in range(COPIES):
                    pool.wait_ge(added[c], 16 * NG * GT // COPIES)

            @block.vector
            def _(dve):
                link = Chain(dve, dve_step)
                v = nc.vector

                def body(i):
                    link.enter(i, 3 * GB)
                    for q in range(GB):
                        link(v.tensor_copy(cols_s[:, q, :, :], cols[:, ds(i * GB + q, 1), :, :].rearrange("p g f j -> p (g f) j")))
                        await_turn(dve, summed, i, PT, PAIRS * (q + 1) - PT)
                        v.tensor_copy(dst_i[:, q, :], cols_s[:, q, DST, :]).then_inc(dst_ready, 1)
                        await_turn(dve, mixed, i, PT, PAIRS * (q + 1) - PT)
                        dve.wait_ge(src_b_in[q], i * 16 + 16)
                        for j in range(GT):
                            s = v.scalar_tensor_tensor(merge[:, q, j, :], src_b[:, q, j * P:(j + 1) * P], cols_s[:, q, SRC, j:j + 1], before[:],
                                                       ALU.is_equal, ALU.mult, accum_out=dup[:, q, j:j + 1])
                        link(s)
                        for j in range(GT):
                            v.tensor_scalar(merge[:, q, j, :], src_b[:, q, j * P:(j + 1) * P], cols_s[:, q, SRC, j:j + 1],
                                            cols_s[:, q, WGT, j:j + 1], ALU.is_equal, ALU.mult)
                            v.tensor_scalar(pick[:, q, j, :], iota_f[:], cols_s[:, q, REL, j:j + 1], None,
                                            ALU.is_equal).then_inc(pick_ready, 1)
                        link(v.scalar_tensor_tensor(row_f[:, q, :], dup[:, q, :], 0.0, cols_s[:, q, OFF, :], ALU.is_equal, ALU.mult))
                        for c in range(COPIES):
                            per = 16 * GB * GT // COPIES
                            await_turn(dve, added[c], i, per, 16 * GT // COPIES * (q + 1) - per)
                        v.tensor_scalar(row_i[:, q, :], row_f[:, q, :], junk_row[:], None, ALU.add).then_inc(rows_ready, 1)
                turns(dve, body)

            @block.tensor
            def _(pe):
                def sums(i, k, slow):
                    q = k // PAIRS
                    if k % PAIRS == 0:
                        pe.wait_ge(h_in[q], i * 16 + 16)
                    pe.wait_ge(mix_ready, i * PT + (k + 1))
                    await_turn(pe, msg_ready, i, PT, k + 1 - 4)
                    for e in range(2):
                        j = (2 * k + e) % GT
                        s = nc.tensor.matmul(bk[2 + k % 4][:, e * D:(e + 1) * D], mix[:, k % 2, e, :],
                                             h_buf[:, q, ds(slow * j, 1), :].rearrange("p j d -> p (j d)"), start=True, stop=True)
                    s.then_inc(summed, 1)


                def body(i):
                    prev = i - 1
                    slow = None
                    for k in range(PT):
                        q = k // PAIRS
                        pe.wait_ge(pick_ready, i * (GB * GT) + (2 * k + 2))
                        await_turn(pe, mix_ready, i, PT, k + 1 - 2)
                        for e in range(2):
                            j = (2 * k + e) % GT
                            s = nc.tensor.matmul(bk[k % 2][:, e * P:(e + 1) * P], pick[:, q, j, :], merge[:, q, j, :], start=True, stop=True)
                        s.then_inc(mixed, 1)
                        if k == 0:
                            if isinstance(i, int):
                                pass
                            else:
                                sl = pe.value_load(table_i[0:1, ds(i * (2 * GB) - 1, 1)], min_val=0, max_val=1)
                                sums(prev, PT - 1, sl)
                        else:
                            if (k - 1) % PAIRS == 0:
                                slow = pe.value_load(table_i[0:1, ds(i * (2 * GB) + (2 * ((k - 1) // PAIRS) + 1), 1)], min_val=0, max_val=1)
                            sums(i, k - 1, slow)
                turns(pe, body)
                sl = pe.value_load(table_i[0:1, 2 * NG - 1:2 * NG], min_val=0, max_val=1)
                sums(GTURNS - 1, PT - 1, sl)

            @block.scalar
            def _(act):
                def take_msg(i, k):
                    act.wait_ge(summed, i * PT + (k + 1))
                    for c in ((2 * k) % COPIES, (2 * k + 1) % COPIES):
                        per = 16 * GB * GT // COPIES
                        await_turn(act, added[c], i, per, 16 * ((2 * k - 8) // COPIES + 1))
                    act.activation(msg[:, k % 4, :, :], bk[2 + k % 4][:, 0:2 * D].rearrange("p (e d) -> p e d", e=2),
                                   ACT.Copy).then_inc(msg_ready, 1)

                def body(i):
                    for k in range(PT):
                        act.wait_ge(mixed, i * PT + (k + 1))
                        await_turn(act, summed, i, PT, k + 1 - 2)
                        act.activation(mix[:, k % 2, :, :], bk[k % 2][:, 0:2 * P].rearrange("p (e m) -> p e m", e=2),
                                       ACT.Copy).then_inc(mix_ready, 1)
                        if k > 0:
                            take_msg(i, k - 1)
                        elif not isinstance(i, int):
                            take_msg(i - 1, PT - 1)
                turns(act, body)
                take_msg(GTURNS - 1, PT - 1)

        layer1.close()

        def window_turns(engine, body):
            body(0, 0, 2)
            with engine.Fori(0, (WT - 3) // 2) as i:
                body(i * 2 + 1, 1, 2)
                body(i * 2 + 2, 0, 2)
            body(WT - 2, 1, 1)
            body(WT - 1, 0, 0)

        gate_stage = ctx.enter_context(ExitStack())

        def sb(name, shape, dt):
            return gate_stage.enter_context(nc.sbuf_tensor(name, shape, dt))

        K2 = 2 * WB
        parts = [[sb(f"part{c}_{q}", [P, WB, D], fp32) for c in range(1, COPIES)] for q in range(2)]
        stats2 = sb("stats2", [P, WB, 6], fp32)
        mv2 = sb("mv2", [P, WB, 2], fp32)
        std2 = sb("std2", [P, WB], fp32)
        xg = sb("xg", [P, WB, D], fp32)
        xr = [sb(f"xr{q}", [P, WB, RW], fp32) for q in range(2)]
        xrT = sb("xrT", [P, 2, NB, P], fp32)
        logits = sb("logits", [P, WB, EX], fp32)
        top8 = sb("top8", [P, WB, 8], fp32)
        idx8 = sb("idx8", [P, WB, 8], u32)
        choice = sb("choice", [P, WB, 2], fp32)
        hot_f = sb("hot_f", [P, K2, EX], fp32)
        hot = sb("hot", [P, K2, EX], bf16)
        hot_sum = sb("hot_sum", [P, EX], fp32)
        ranks = sb("ranks", [P, K2, EX], fp32)
        slot_f = sb("slot_f", [P, K2], fp32)
        slot_i = sb("slot_i", [P, 2, K2], i32)
        gap = sb("gap", [P, NW], fp32)
        ratio = sb("ratio", [P, NW], fp32)
        total = sb("total", [P, NW], fp32)

        x1_in = [[sem(f"x1_in{c}_{q}") for c in range(COPIES)] for q in range(2)]
        parts_summed = sem("parts_summed")
        x1_ready = sem("x1_ready")
        mv2_ready = sem("mv2_ready")
        std2_ready = sem("std2_ready")
        norm2_ready = sem("norm2_ready")
        xg_ready = sem("xg_ready")
        xr_ready = sem("xr_ready")
        xr_turned = sem("xr_turned")
        xrT_ready = sem("xrT_ready")
        gated = sem("gated")
        logits_taken = sem("logits_taken")
        hot_ready = sem("hot_ready")
        ranked = sem("ranked")
        slots_ready = sem("slots_ready")
        sent = [sem(f"sent{q}") for q in range(2)]
        gate_own = sem("gate_own")
        counted = sem("counted")
        counts_ready = sem("counts_ready")
        tiles_ready = sem("tiles_ready")
        fill_set = sem("fill_set")
        filled = sem("filled")
        gap_ready = sem("gap_ready")
        ratio_ready = sem("ratio_ready")

        with nc.Block() as block:
            @block.sync
            def _(sp):
                def body(t, q, more):
                    await_turn(sp, x1_ready, t, 1, -1)
                    for c in range(COPIES):
                        to = x1[:, ds(t * WB, WB), :] if c == 0 else parts[q][c - 1][:]
                        sp.dma_start(to, acc[c][ds(t * (WB * P), WB * P), :].rearrange("(w p) d -> p w d", p=P)).then_inc(x1_in[q][c], 16)
                window_turns(sp, body)
                sp.wait_ge(counts_ready, 1)
                with sp.Fori(0, EX // 2) as i:
                    for q in range(2):
                        e = i * 2 + q
                        count = sp.value_load(counts_i[0:1, ds(e, 1)], min_val=0, max_val=NP)
                        sp.dma_start(slots_dram[ds(e * CAP + count, P), :], filler[:, q, :]).then_inc(filled, 16)
                sp.wait_ge(filled, 16 * EX)

            @block.gpsimd
            def _(pool):
                def body(t, q, more):
                    pool.wait_ge(slots_ready, t + 1)
                    pool.wait_ge(xr_ready, t + 1)
                    pool.sem_inc(pool_steps, 1)
                    for n in range(K2):
                        pool.indirect_dma_start(slots_dram, bass.IndirectOffsetOnAxis(ap=slot_i[:, q, n:n + 1], axis=0),
                                                xr[q][:, n // 2, :], None).then_inc(sent[q], 16)
                window_turns(pool, body)
                pool.wait_ge(sent[0], 16 * K2 * ((WT + 1) // 2))
                pool.wait_ge(sent[1], 16 * K2 * (WT // 2))

            @block.scalar
            def _(act):
                def deviations(t):
                    act.wait_ge(mv2_ready, t + 1)
                    act.activation(std2[:], mv2[:, :, 1], ACT.Sqrt, bias=eps[:]).then_inc(std2_ready, 1)

                def norm(to, t, j):
                    w = t * WB + j
                    return act.activation(to, x1[:, ds(w, 1), :].rearrange("p w d -> p (w d)"), ACT.Identity,
                                          bias=shift2[:, ds(w, 1)], scale=rstd2[:, ds(w, 1)])

                def rows(t, q):
                    await_turn(act, sent[q], t, 8 * K2, -8 * K2 * q)
                    act.sem_inc(act_steps, 1)
                    for j in range(WB):
                        s = norm(xr[q][:, j, 0:D], t, j)
                    s.then_inc(xr_ready, 1)

                def body(t, q, more):
                    act.wait_ge(norm2_ready, t + 1)
                    await_turn(act, xr_turned, t, WB, 0)
                    act.sem_inc(act_steps, 1)
                    for j in range(WB):
                        norm(xg[:, j, :], t, j).then_inc(xg_ready, 1)
                    for j in range(WB):
                        act.wait_ge(xr_turned, t * WB + (j + 1))
                        await_turn(act, gated, t, WB, j - 1)
                        act.activation(xrT[:, j % 2, :, :], bk[j % 2][:, 0:D].rearrange("p (b n) -> p b n", b=NB),
                                       ACT.Copy).then_inc(xrT_ready, 1)
                    if more > 0:
                        deviations(t + 1)
                    rows(t, q)
                deviations(0)
                window_turns(act, body)
                act.wait_ge(gap_ready, 1)
                act.activation(ratio[:], gap[:], ACT.Exp).then_inc(ratio_ready, 1)

            @block.tensor
            def _(pe):
                def turn_window(t, j):
                    pe.wait_ge(xg_ready, t * WB + (j + 1))
                    await_turn(pe, xrT_ready, t, WB, j - 1)
                    for b in range(NB):
                        s = nc.tensor.transpose(bk[j % 2][:, b * P:(b + 1) * P], xg[:, j, b * P:(b + 1) * P], ident[:])
                    s.then_inc(xr_turned, 1)

                def sum_parts(t, q):
                    for c in range(2, COPIES):
                        pe.wait_ge(x1_in[q][c], t * 8 + (16 - 8 * q))
                    await_turn(pe, x1_ready, t, 1, 0)
                    pe.sem_inc(pe_steps, 1)
                    for j in range(WB):
                        for c in range(2, COPIES):
                            s = nc.tensor.matmul(bk[4 + j // 2][:, (j % 2) * D:(j % 2 + 1) * D], ident[:], parts[q][c - 1][:, j, :],
                                                 start=c == 2, stop=c == COPIES - 1)
                        s.then_inc(parts_summed, 1)

                def body(t, q, more):
                    await_turn(pe, logits_taken, t, 1, 0)
                    turn_window(t, 0)
                    for j in range(WB):
                        if j + 1 < WB:
                            turn_window(t, j + 1)
                        pe.wait_ge(xrT_ready, t * WB + (j + 1))
                        for b in range(NB):
                            s = nc.tensor.matmul(bk[2][:, j * EX:(j + 1) * EX], xrT[:, j % 2, b, :], gate_sb[:, b, :],
                                                 start=b == 0, stop=b == NB - 1)
                        s.then_inc(gated, 1)
                    starts = isinstance(t, int) and t == 0
                    if more == 2 and not starts:
                        sum_parts(t + 2, q)
                    pe.wait_ge(hot_ready, t + 1)
                    nc.tensor.matmul(bk[3][:, 0:K2 * EX], upper[:], hot[:].rearrange("p n e -> p (n e)"),
                                     start=True, stop=False, skip_group_check=True)
                    for n in range(1, K2):
                        nc.tensor.matmul(bk[3][:, n * EX:K2 * EX], ones_b[:], hot[:, 0:K2 - n, :].rearrange("p n e -> p (n e)"),
                                         start=False, stop=False, skip_group_check=True)
                    nc.tensor.matmul(bk[3][:, 0:K2 * EX].rearrange("p (n e) -> p n e", e=EX), ones_b[:],
                                     carry[:, None, :].to_broadcast([P, K2, EX]),
                                     start=False, stop=True, skip_group_check=True).then_inc(ranked, 1)
                    if starts:
                        sum_parts(2, 0)
                sum_parts(0, 0)
                sum_parts(1, 1)
                window_turns(pe, body)
                pe.wait_ge(counted, 1)
                nc.tensor.matmul(bk[0][0:1, 0:EX], ones_b[:, 0:1], carry[:], start=True, stop=True).then_inc(counted, 1)

            @block.vector
            def _(dve):
                link = Chain(dve, gate_own)
                v = nc.vector

                def sum_and_measure(t, q):
                    for c in range(2):
                        dve.wait_ge(x1_in[q][c], t * 8 + (16 - 8 * q))
                    here = x1[:, ds(t * WB, WB), :]
                    link(v.tensor_tensor(here, here, parts[q][0][:], ALU.add))
                    for j in range(0, WB, 2):
                        n = min(2, WB - j)
                        dve.wait_ge(parts_summed, t * WB + (j + n))
                        here = x1[:, ds(t * WB + j, n), :]
                        s = v.tensor_tensor(here, here, bk[4 + j // 2][:, 0:n * D].rearrange("p (w d) -> p w d", d=D), ALU.add)
                    link(s)
                    dve.sem_inc(x1_ready, 1)
                    for j in range(WB):
                        s = v.bn_stats(stats2[:, j, :], x1[:, ds(t * WB + j, 1), :].rearrange("p w d -> p (w d)"))
                    link(s)
                    dve.sem_inc(dve_steps, 1)
                    for j in range(WB):
                        s = v.bn_aggr(mv2[:, j, :], stats2[:, j, :])
                    s.then_inc(mv2_ready, 1)

                def norm_factors(t):
                    dve.wait_ge(std2_ready, t + 1)
                    rs, sh = rstd2[:, ds(t * WB, WB)], shift2[:, ds(t * WB, WB)]
                    link(v.reciprocal(rs, std2[:]))
                    link(v.scalar_tensor_tensor(sh, mv2[:, :, 0], -1.0, rs, ALU.mult, ALU.mult))
                    dve.sem_inc(norm2_ready, 1)

                def body(t, q, more):
                    starts = isinstance(t, int) and t == 0
                    if more == 2:
                        link.enter(t, 16)
                    elif more == 1:
                        link.leave(WT - 2)
                    if more > 0:
                        norm_factors(t + 1)
                    dve.wait_ge(gated, t * WB + WB)
                    s = v.tensor_tensor(logits[:], bk[2][:, 0:WB * EX].rearrange("p (w e) -> p w e", e=EX),
                                        gate_bb[:, None, :].to_broadcast([P, WB, EX]), ALU.add)
                    link(s)
                    dve.sem_inc(logits_taken, 1)
                    for j in range(WB):
                        s = v.max(top8[:, j, :], logits[:, j, :])
                    link(s)
                    dve.sem_inc(dve_steps, 1)
                    for j in range(WB):
                        s = v.max_index(idx8[:, j, :], top8[:, j, :], logits[:, j, :])
                    link(s)
                    v.tensor_copy(top2[:, ds(t * WB, WB), :], top8[:, :, 0:2])
                    link(v.tensor_copy(choice[:], idx8[:, :, 0:2]))
                    for k in range(2):
                        s = v.tensor_tensor(hot_f[:].rearrange("p (w k) e -> p w k e", k=2)[:, :, k, :],
                                            iota_f[:, None, 0:EX].to_broadcast([P, WB, EX]),
                                            choice[:, :, k:k + 1].to_broadcast([P, WB, EX]), ALU.is_equal)
                    link(s)
                    v.tensor_reduce(hot_sum[:], hot_f[:].rearrange("p n e -> p e n"), AX.X, ALU.add)
                    link(v.tensor_copy(hot[:], hot_f[:]))
                    dve.sem_inc(hot_ready, 1)
                    if more == 2 and not starts:
                        sum_and_measure(t + 2, q)
                    dve.wait_ge(ranked, t + 1)
                    link(v.tensor_tensor(ranks[:], bk[3][:, 0:K2 * EX].rearrange("p (n e) -> p n e", e=EX),
                                         expert_base[:, None, :].to_broadcast([P, K2, EX]), ALU.add))
                    link(v.tensor_tensor(ranks[:], ranks[:], hot_f[:], ALU.mult))
                    v.tensor_tensor(carry_f[:], carry_f[:], hot_sum[:], ALU.add)
                    link(v.tensor_reduce(slot_f[:], ranks[:], AX.X, ALU.add))
                    v.tensor_copy(carry[:], carry_f[:])
                    await_turn(dve, sent[q], t, 8 * K2, -8 * K2 * q)
                    v.tensor_copy(xr[q][:, :, TOKEN], tok[:])
                    v.tensor_copy(xr[q][:, :, CHOICE], choice[:, :, 0])
                    link(v.tensor_copy(slot_i[:, q, :], slot_f[:]))
                    link(v.tensor_scalar(tok[:], tok[:], float(WB * P), None, ALU.add))
                    dve.sem_inc(slots_ready, 1)
                    if starts:
                        sum_and_measure(2, 0)
                for q in range(2):
                    v.memset(xr[q][:, :, D:RW], 0.0)
                v.memset(carry_f[:], 0.0)
                v.memset(carry[:], 0.0)
                link(v.memset(filler[:], 0.0))
                for j in range(WB):
                    v.tensor_scalar(tok[:, j:j + 1], part_f[:], float(j * P), None, ALU.add)
                v.tensor_scalar(expert_base[:], iota_f[:, 0:EX], float(CAP), None, ALU.mult)
                for q in range(2):
                    v.tensor_scalar(filler[:, q, TOKEN:TOKEN + 1], part_f[:], float(NP + q * P), None, ALU.add)
                link(v.memset(filler[:, :, CHOICE:CHOICE + 1], -1.0))
                sum_and_measure(0, 0)
                norm_factors(0)
                sum_and_measure(1, 1)
                window_turns(dve, body)
                dve.sem_inc(counted, 1)
                dve.wait_ge(counted, 2)
                link(v.tensor_copy(counts_f[:], bk[0][0:1, 0:EX]))
                v.tensor_copy(counts_i[:], counts_f[:]).then_inc(counts_ready, 1)
                link(v.tensor_scalar(ntiles_i[:], counts_f[:], float(P - 1), None, ALU.add))
                link(v.tensor_scalar(ntiles_i[:], ntiles_i[:], P.bit_length() - 1, None, ALU.arith_shift_right))
                link(v.tensor_scalar(ntiles_f[:], ntiles_i[:], 1.0, None, ALU.max))
                link(v.tensor_tensor_scan(ends_f[:], ones[0:1, 0:EX], ntiles_f[:], 0.0, ALU.mult, ALU.add))
                v.memset(tiles_i[:, 0:1], 0)
                link(v.tensor_copy(tiles_i[:, 1:EX + 1], ends_f[:]))
                v.tensor_tensor(gap[:], top2[:, :, 1], top2[:, :, 0], ALU.subtract).then_inc(gap_ready, 1)
                dve.wait_ge(ratio_ready, 1)
                link(v.tensor_scalar(total[:], ratio[:], 1.0, None, ALU.add))
                link(v.reciprocal(first_w[:], total[:]))
                link(v.tensor_tensor(second_w[:], ratio[:], first_w[:], ALU.mult))
        gate_stage.close()

        xn2 = ctx.enter_context(nc.sbuf_tensor("xn2", [P, NW, D], fp32))
        expert_stage = ctx.enter_context(ExitStack())

        def sb(name, shape, dt):
            return expert_stage.enter_context(nc.sbuf_tensor(name, shape, dt))

        xt = sb("xt", [P, RW], fp32)
        xtT = sb("xtT", [P, NB, P], fp32)
        held = sb("held", [P, 2], fp32)
        other = sb("other", [P, 1], fp32)
        to_i = sb("to_i", [P, 2, 1], i32)
        start_i = sb("start_i", [P, 3], i32)
        hT = sb("hT", [P, FB, P], fp32)
        y_sb = sb("y_sb", [P, 2, D], fp32)

        xt_in = sem("xt_in")
        xt_turned = sem("xt_turned")
        xt_read = sem("xt_read")
        xtT_ready = sem("xtT_ready")
        up_done = sem("up_done")
        hT_ready = sem("hT_ready")
        down_done = sem("down_done")
        y_ready = sem("y_ready")
        y_sent = [sem(f"y_sent{q}") for q in range(2)]
        xn2_ready = sem("xn2_ready")
        first_set = sem("first_set")
        expert_own = sem("expert_own")

        def experts(engine, start, tile, end):
            with engine.Fori(0, EX // 2) as i:
                for q in range(2):
                    e = i * 2 + q
                    lo = engine.value_load(tiles_i[0:1, ds(e, 1)], min_val=0, max_val=MAXT)
                    hi = engine.value_load(tiles_i[0:1, ds(e + 1, 1)], min_val=1, max_val=MAXT)
                    start(i, e, q)
                    with engine.Fori(lo, hi) as s:
                        tile(i, e, q, s, lo)
                    end(i, e, q, hi)

        MAXT = 2 * NP // P + EX
        WE = NW // EX

        def nothing(*_):
            pass

        with nc.Block() as block:
            @block.sync
            def _(sp):
                def tile(i, e, q, s, lo):
                    sp.wait_ge(xt_turned, s + 1)
                    sp.wait_ge(xt_read, s + 1)
                    sp.dma_start(xt[:], slots_dram[ds((e * CAP + (s - lo) * P).with_bounds(min_val=0, max_val=EX * CAP - P), P), :]).then_inc(xt_in, 16)

                def end(i, e, q, hi):
                    pass
                experts(sp, nothing, tile, end)
                tiles = sp.value_load(tiles_i[0:1, EX:EX + 1], min_val=EX, max_val=MAXT)
                sp.wait_ge(xt_turned, tiles + 1)
                sp.wait_ge(xt_read, tiles + 1)
                sp.dma_start(xt[:], slots_dram[0:P, :]).then_inc(xt_in, 16)
                sp.wait_ge(xt_in, tiles * 16 + 16)
                sp.sem_inc(sp_steps, 1)

            @block.gpsimd
            def _(pool):
                pool.wait_ge(first_set, 1)
                for n in range(3):
                    if n == 2:
                        pool.wait_ge(y_sent[1], 16)
                    pool.indirect_dma_start(y_dram, bass.IndirectOffsetOnAxis(ap=start_i[:, n:n + 1], axis=0),
                                            y_sb[:, min(n, 1), :], None).then_inc(y_sent[min(n, 1)], 16)

                def tile(i, e, q, s, lo):
                    pool.wait_ge(y_ready, s + 2)
                    pool.sem_inc(pool_steps, 1)
                    with pool.If((s & 1) == 0):
                        pool.indirect_dma_start(y_dram, bass.IndirectOffsetOnAxis(ap=to_i[:, 0, :], axis=0),
                                                y_sb[:, 0, :], None).then_inc(y_sent[0], 16)
                    with pool.Else():
                        pool.indirect_dma_start(y_dram, bass.IndirectOffsetOnAxis(ap=to_i[:, 1, :], axis=0),
                                                y_sb[:, 1, :], None).then_inc(y_sent[1], 16)
                    pool.nop()
                experts(pool, nothing, tile, nothing)
                tiles = pool.value_load(tiles_i[0:1, EX:EX + 1], min_val=EX, max_val=MAXT)
                pool.wait_ge(y_sent[0], ((tiles + 1) >> 1) * 16 + 16)
                pool.wait_ge(y_sent[1], (tiles >> 1) * 16 + 32)

            @block.scalar
            def _(act):
                act.sem_inc(hT_ready, 1)

                def norm_input(w):
                    act.activation(xn2[:, ds(w, 1), :].rearrange("p w d -> p (w d)"), x1[:, ds(w, 1), :].rearrange("p w d -> p (w d)"),
                                   ACT.Identity, bias=shift2[:, ds(w, 1)], scale=rstd2[:, ds(w, 1)]).then_inc(xn2_ready, 1)

                def start(i, e, q):
                    for n in range(WE):
                        norm_input(e * WE + n)

                def tile(i, e, q, s, lo):
                    act.wait_ge(down_done, s + 1)
                    for f in range(FB):
                        act.wait_ge(up_done, s * FB + (f + 1))
                        act.activation(hT[:, f, :], bk[f][:, 0:P], ACT.Relu,
                                       bias=b1_cols[:, ds(e * FB + f, 1)]).then_inc(hT_ready, 1)

                def end(i, e, q, hi):
                    act.wait_ge(down_done, hi + 1)
                    act.sem_inc(sp_steps, 1)
                    with act.If(i < EX // 2 - 1):
                        load_expert(act, (e + 2).with_bounds(min_val=2, max_val=EX - 1), q)
                    act.nop()
                experts(act, start, tile, end)
                for n in range(WE * EX, NW):
                    norm_input(n)

            @block.tensor
            def _(pe):
                def turn_tile():
                    for b in range(NB):
                        s = nc.tensor.transpose(bk[4][:, b * P:(b + 1) * P], xt[:, b * P:(b + 1) * P], ident[:])
                    s.then_inc(xt_turned, 1)

                pe.sem_inc(down_done, 1)
                pe.sem_inc(xt_turned, 1)
                pe.wait_ge(xt_in, 16)
                turn_tile()

                def start(i, e, q):
                    pe.wait_ge(w_expert_in[q], i * 32 + 32)
                    pe.sem_inc(pe_steps, 1)

                def tile(i, e, q, s, lo):
                    pe.wait_ge(xtT_ready, s + 1)
                    pe.wait_ge(hT_ready, s * FB + 1)
                    for f in range(FB):
                        for b in range(NB):
                            m = nc.tensor.matmul(bk[f][:, 0:P], w1_sb[:, q, b, f * P:(f + 1) * P], xtT[:, b, :],
                                                 start=b == 0, stop=b == NB - 1)
                        m.then_inc(up_done, 1)
                    pe.wait_ge(xt_in, s * 16 + 32)
                    turn_tile()
                    pe.wait_ge(y_ready, s + 1)
                    for f in range(FB):
                        pe.wait_ge(hT_ready, s * FB + (f + 2))
                        m = nc.tensor.matmul(bk[5][:, 0:D], hT[:, f, :], w2_sb[:, q, f, :], start=f == 0, stop=f == FB - 1)
                    m.then_inc(down_done, 1)
                experts(pe, start, tile, nothing)

            @block.vector
            def _(dve):
                link = Chain(dve, expert_own)
                v = nc.vector

                def take_tile():
                    v.tensor_copy(held[:], xt[:, TOKEN:CHOICE + 1]).then_inc(xt_read, 1)
                    v.tensor_copy(xtT[:], bk[4][:, 0:D].rearrange("p (b n) -> p b n", b=NB)).then_inc(xtT_ready, 1)

                dve.sem_inc(xt_read, 1)
                dve.sem_inc(y_ready, 1)
                link(v.memset(y_sb[:], 0.0))
                for n in range(3):
                    s = v.tensor_scalar(start_i[:, n:n + 1], part_f[:], float(2 * NP + (2 + n) * P), None, ALU.add)
                s.then_inc(first_set, 1)
                dve.wait_ge(xt_turned, 2)
                take_tile()

                def add_beta(w, n):
                    dve.wait_ge(xn2_ready, w + n)
                    here = x1[:, ds(w, n), :]
                    v.tensor_tensor(here, here, beta_b[:, None, :].to_broadcast([P, n, D]), ALU.add)

                def end(i, e, q, hi):
                    add_beta(e * WE, WE)

                def tile(i, e, q, s, lo):
                    dve.wait_ge(xt_read, s + 2)
                    v.tensor_scalar(other[:], held[:, 1:2], iota_f[:, ds(e, 1)], float(NP), ALU.not_equal, ALU.mult).then_inc(expert_own, 1)
                    dve.wait_ge(expert_own, s * 2 + 2)
                    dve.wait_ge(y_sent[0], (s >> 1) * 16 + 16)
                    dve.wait_ge(y_sent[1], ((s + 1) >> 1) * 16 + 16)
                    v.tensor_tensor(to_i[:, ds(s & 1, 1), :].rearrange("p a b -> p (a b)"), other[:], held[:, 0:1], ALU.add).then_inc(expert_own, 1)
                    dve.wait_ge(expert_own, s * 2 + 3)
                    dve.wait_ge(xt_turned, s + 3)
                    dve.wait_ge(up_done, s * FB + FB)
                    take_tile()
                    dve.wait_ge(down_done, s + 2)
                    v.tensor_tensor(y_sb[:, ds(s & 1, 1), :].rearrange("p a d -> p (a d)"), bk[5][:, 0:D], b2_b[:, ds(e, 1), :].rearrange("p e d -> p (e d)"), ALU.add).then_inc(y_ready, 1)
                experts(dve, nothing, tile, end)
                add_beta(WE * EX, NW - WE * EX)
        expert_stage.close()

        last_stage = ctx.enter_context(ExitStack())

        def sb(name, shape, dt):
            return last_stage.enter_context(nc.sbuf_tensor(name, shape, dt))

        ya = [sb(f"ya{q}", [P, WB, D], fp32) for q in range(2)]
        yb = [sb(f"yb{q}", [P, WB, D], fp32) for q in range(2)]
        o = [sb(f"o{q}", [P, WB, D], fp32) for q in range(2)]
        stats3 = sb("stats3", [P, WB, 6], fp32)
        mv3 = sb("mv3", [P, WB, 2], fp32)
        std3 = sb("std3", [P, WB], fp32)
        rs3 = sb("rs3", [P, WB], fp32)
        sh3 = sb("sh3", [P, WB], fp32)

        LATE = 2
        y_in = [sem(f"y_in{q}") for q in range(2)]
        y_summed = sem("y_summed")
        mv3_ready = sem("mv3_ready")
        std3_ready = sem("std3_ready")
        norm3_ready = sem("norm3_ready")
        yn_ready = sem("yn_ready")
        last_ready = sem("last_ready")
        scaled = sem("scaled")
        out_ready = sem("out_ready")
        out_sent = [sem(f"out_sent{q}") for q in range(2)]
        last_own = sem("last_own")

        with nc.Block() as block:
            @block.sync
            def _(sp):
                def load(t, q):
                    for k, to in enumerate((ya[q], yb[q])):
                        sp.dma_start(to[:], y_dram[ds(t * (WB * P) + k * NP, WB * P), :].rearrange("(w p) d -> p w d", p=P)).then_inc(y_in[q], 16)

                def body(t, q, more):
                    if more == 2:
                        sp.wait_ge(y_summed, t + 1)
                        load(t + 2, q)
                    if more > 0:
                        sp.wait_ge(out_ready, t + 1)
                        sp.dma_start(out[ds(t * (WB * P), WB * P), :].rearrange("(w p) d -> p w d", p=P), o[q][:]).then_inc(out_sent[q], 16)
                load(0, 0)
                load(1, 1)
                window_turns(sp, body)
                w0 = (WT - 1) * WB
                sp.wait_ge(out_ready, WT)
                sp.dma_start(out[w0 * P:(w0 + LATE) * P, :].rearrange("(w p) d -> p w d", p=P), o[0][:, 0:LATE, :]).then_inc(out_sent[0], 16)
                sp.wait_ge(last_ready, 1)
                sp.dma_start(out[(w0 + LATE) * P:(NW - 1) * P, :].rearrange("(w p) d -> p w d", p=P), o[0][:, LATE:WB - 1, :]).then_inc(out_sent[0], 16)
                sp.dma_start(out[(NW - 1) * P:N, :], o[0][0:LASTW, WB - 1, :]).then_inc(out_sent[0], 16)
                sp.wait_ge(out_sent[0], 16 * ((WT - 1) // 2 + 3))
                sp.wait_ge(out_sent[1], 16 * (WT // 2))

            @block.scalar
            def _(act):
                def body(t, q, more):
                    act.wait_ge(mv3_ready, t + 1)
                    act.activation(std3[:], mv3[:, :, 1], ACT.Sqrt, bias=eps[:]).then_inc(std3_ready, 1)
                    act.wait_ge(norm3_ready, t + 1)
                    for j in range(WB):
                        s = act.activation(o[q][:, j, :], o[q][:, j, :], ACT.Identity, bias=sh3[:, j:j + 1], scale=rs3[:, j:j + 1])
                    s.then_inc(yn_ready, 1)
                window_turns(act, body)

            @block.gpsimd
            def _(pool):
                def body(t, q, more):
                    n = WB if more else LATE
                    pool.wait_ge(yn_ready, t + 1)
                    pool.tensor_tensor(o[q][:, 0:n, :], o[q][:, 0:n, :], gamma_b[:, None, :].to_broadcast([P, n, D]), ALU.mult).then_inc(scaled, 1)
                    pool.wait_ge(scaled, t + 1)
                    pool.sem_inc(pool_steps, 1)
                    pool.tensor_tensor(o[q][:, 0:n, :], o[q][:, 0:n, :], x1[:, ds(t * WB, n), :], ALU.add).then_inc(out_ready, 1)
                window_turns(pool, body)

            @block.vector
            def _(dve):
                link = Chain(dve, last_own)
                v = nc.vector

                def add_first(t, q):
                    dve.wait_ge(y_in[q], t * 16 + (2 - q) * 16)
                    dve.sem_inc(dve_steps, 1)
                    for j in range(WB):
                        s = v.scalar_tensor_tensor(ya[q][:, j, :], ya[q][:, j, :], first_w[:, ds(t * WB + j, 1)],
                                                   xn2[:, ds(t * WB + j, 1), :].rearrange("p w d -> p (w d)"), ALU.mult, ALU.add)
                    link(s)

                def body(t, q, more):
                    if more == 2:
                        link.enter(t, 5)
                    elif more == 1:
                        link.leave(WT - 2)
                    await_turn(dve, out_sent[q], t, 8, -8 * q)
                    dve.sem_inc(dve_steps, 1)
                    for j in range(WB):
                        s = v.scalar_tensor_tensor(o[q][:, j, :], yb[q][:, j, :], second_w[:, ds(t * WB + j, 1)], ya[q][:, j, :], ALU.mult, ALU.add)
                    link(s)
                    dve.sem_inc(y_summed, 1)
                    for j in range(WB):
                        s = v.bn_stats(stats3[:, j, :], o[q][:, j, :])
                    link(s)
                    dve.sem_inc(dve_steps, 1)
                    for j in range(WB):
                        s = v.bn_aggr(mv3[:, j, :], stats3[:, j, :])
                    s.then_inc(mv3_ready, 1)
                    if more > 0:
                        add_first(t + 1, 1 - q)
                    dve.wait_ge(std3_ready, t + 1)
                    await_turn(dve, yn_ready, t, 1, 0)
                    link(v.reciprocal(rs3[:], std3[:]))
                    link(v.scalar_tensor_tensor(sh3[:], mv3[:, :, 0], -1.0, rs3[:], ALU.mult, ALU.mult))
                    dve.sem_inc(norm3_ready, 1)
                add_first(0, 0)
                window_turns(dve, body)
                late = o[0][:, LATE:WB, :]
                dve.wait_ge(yn_ready, WT)
                link(v.tensor_tensor(late, late, gamma_b[:, None, :].to_broadcast([P, WB - LATE, D]), ALU.mult))
                link(v.tensor_tensor(late, late, x1[:, NW - WB + LATE:NW, :], ALU.add))
                dve.sem_inc(last_ready, 1)
        last_stage.close()


_INS = ['x', 'src', 'dst', 'edge_weight', 'L0_gnn_W', 'L0_ffn_gate_w', 'L0_ffn_gate_b', 'L0_ffn_w1', 'L0_ffn_b1',
        'L0_ffn_w2', 'L0_ffn_b2', 'L0_ffn_gamma', 'L0_ffn_beta']
_OUTS = [((6250, 256), 'float32')]


def kernel(**inputs):
    import numpy as _np
    import concourse.bacc as _bacc
    from concourse import mybir as _mybir
    from concourse.bass_utils import run_bass_kernel_spmd as _run

    nc = _bacc.Bacc("TRN2", target_bir_lowering=False, num_devices=1)
    arrays, args = {}, []
    for name in _INS:
        a = _np.ascontiguousarray(inputs[name])
        arrays[f"in_{name}_dram"] = a
        args.append(nc.dram_tensor(f"in_{name}_dram", a.shape, _mybir.dt.from_np(a.dtype), kind="ExternalInput").ap())
    for i, (shape, dtype) in enumerate(_OUTS):
        dt = _mybir.dt.from_np(_np.dtype(dtype))
        args.append(nc.dram_tensor(f"out_{i}_dram", shape, dt, kind="ExternalOutput").ap())
    gnn_moe_kernel(nc, *args)
    r = _run(nc, [arrays], core_ids=[0])
    got = tuple(r.results[0][f"out_{i}_dram"] for i in range(len(_OUTS)))
    return got[0]
```

```python
import concourse.bass as bass
from concourse import mybir
from contextlib import ExitStack


class Chain:

    def __init__(self, engine, done):
        self.engine, self.done, self.base, self.n, self.per, self.turn = engine, done, 0, 0, 0, 0

    def enter(self, turn, per):
        if not self.per:
            self.base += self.n
        self.turn, self.per, self.n = turn, per, 0

    def leave(self, turns):
        assert self.n == self.per, (self.n, self.per)
        self.base, self.per, self.turn, self.n = self.base + turns * self.per, 0, 0, 0

    def __call__(self, instruction):
        instruction.then_inc(self.done, 1)
        self.n += 1
        self.engine.wait_ge(self.done, self.turn * self.per + (self.base + self.n))


def await_turn(engine, sem, turn, per, value):
    if isinstance(turn, int):
        if per * turn + value > 0:
            engine.wait_ge(sem, per * turn + value)
    else:
        engine.wait_ge(sem, turn * per + value)


def gnn_moe_kernel(nc, x, src, dst, edge_weight, gnn_w, gate_w, gate_b, w1, b1, w2, b2, gamma, beta, out):
    fp32, bf16, i32, u32 = mybir.dt.float32, mybir.dt.bfloat16, mybir.dt.int32, mybir.dt.uint32
    ALU, ACT, AX = mybir.AluOpType, mybir.ActivationFunctionType, mybir.AxisListType
    ds = bass.ds

    P = 128
    N, D = x.shape
    NE = src.shape[0]
    EX, _, F = w1.shape
    EPS = 1e-5
    NB = D // P
    NW = -(-N // P)
    WB = 7
    WT = NW // WB
    assert WB * WT == NW
    NP = NW * P
    LASTW = N - (NW - 1) * P
    GT = 8
    GE = GT * P
    NG = -(-NE // GE)
    NG += NG % 2
    FULL = NE // GE
    REST = NE - FULL * GE
    COPIES = 4
    JUNK = NP
    ROWS = NP + P
    GB = 2
    GTURNS = NG // GB
    PAIRS = GT // 2
    PT = GB * PAIRS
    LAG = 3

    FB = F // P
    MAXT = 2 * NP // P + EX
    NWT = MAXT // 2 + 1
    CAP = NP + P
    RW = 264
    TOKEN, CHOICE = D, D + 1
    slots_dram = nc.dram_tensor("slots", [EX * CAP, RW], fp32).ap()
    y_dram = nc.dram_tensor("expert_out", [2 * NP + 5 * P, D], fp32).ap()
    h_rows_dram = nc.dram_tensor("h_rows", [NP, D], fp32).ap()
    src_dram = nc.dram_tensor("src_padded", [NG, GE], i32).ap()
    table_dram = nc.dram_tensor("group_table", [NG, 2], fp32).ap()
    acc = [nc.dram_tensor(f"acc{c}", [ROWS, D], fp32).ap() for c in range(COPIES)]

    ctx = ExitStack()
    with ctx:
        def sb(name, shape, dt):
            return ctx.enter_context(nc.sbuf_tensor(name, shape, dt))

        def bank(name, shape, dt=fp32):
            return ctx.enter_context(nc.psum_tensor(name, shape, dt))

        def sem(name):
            return ctx.enter_context(nc.semaphore(name))

        ones = sb("ones", [P, P], fp32)
        ident = sb("ident", [P, P], fp32)
        iota_i = sb("iota_i", [P, P], i32)
        iota_f = sb("iota_f", [P, P], fp32)
        part_i = sb("part_i", [P, 1], i32)
        part_f = sb("part_f", [P, 1], fp32)
        junk_row = sb("junk_row", [P, 1], fp32)
        before = sb("before", [P, P], fp32)
        eps = sb("eps", [P, 1], fp32)

        x1 = sb("x1", [P, NWT, D], fp32)
        rstd2 = sb("rstd2", [P, NWT], fp32)
        shift2 = sb("shift2", [P, NWT], fp32)
        top2 = sb("top2", [P, NW, 2], fp32)
        first_w = sb("first_w", [P, NW], fp32)
        second_w = sb("second_w", [P, NW], fp32)
        upper = sb("upper", [P, P], bf16)
        ones_b = sb("ones_b", [P, P], bf16)
        gate_sb = sb("gate_sb", [P, NB, EX], fp32)
        gate_bb = sb("gate_bb", [P, EX], fp32)
        expert_base = sb("expert_base", [P, EX], fp32)
        carry = sb("carry", [P, EX], bf16)
        carry_f = sb("carry_f", [P, EX], fp32)
        filler = sb("filler", [P, 2, RW], fp32)
        tok = sb("tok", [P, WB], fp32)
        counts_f = sb("counts_f", [1, EX], fp32)
        counts_i = sb("counts_i", [1, EX], i32)
        ntiles_i = sb("ntiles_i", [1, EX], i32)
        ntiles_f = sb("ntiles_f", [1, EX], fp32)
        ends_f = sb("ends_f", [1, EX], fp32)
        tiles_i = sb("tiles_i", [1, EX + 1], i32)
        w1_sb = sb("w1_sb", [P, 2, NB, F], fp32)
        w2_sb = sb("w2_sb", [P, 2, FB, D], fp32)
        b1_rows = sb("b1_rows", [EX * FB, P], fp32)
        b1_cols = sb("b1_cols", [P, EX * FB], fp32)
        b2_b = sb("b2_b", [P, EX, D], fp32)
        gamma_b = sb("gamma_b", [P, D], fp32)
        beta_b = sb("beta_b", [P, D], fp32)

        layer1 = ctx.enter_context(ExitStack())

        def sb(name, shape, dt):
            return layer1.enter_context(nc.sbuf_tensor(name, shape, dt))

        table_b = sb("table_b", [P, NG, 2], fp32)
        table_i = sb("table_i", [1, NG * 2], i32)
        gathers_i = sb("gathers_i", [1, NG], i32)
        SRC, WGT, REL, OFF, DST = range(5)
        cols = sb("cols", [P, NG, 5, GT], fp32)
        src_b = sb("src_b", [P, GB, GE], i32)
        zeros = sb("zeros", [P, 10 * D], fp32)

        prepare = ctx.enter_context(ExitStack())

        def sb(name, shape, dt):
            return prepare.enter_context(nc.sbuf_tensor(name, shape, dt))

        stats = sb("stats", [P, NW, 6], fp32)
        mv = sb("mv", [P, NW, 2], fp32)
        upper_f = sb("upper_f", [P, P], fp32)
        std = sb("std", [P, NW], fp32)
        rstd = sb("rstd", [P, NW], fp32)
        shift = sb("shift", [P, NW], fp32)
        xn = sb("xn", [P, WB, D], fp32)
        xnT = sb("xnT", [P, WB, NB, P], fp32)
        w_rows = sb("w_rows", [P, NB, D], fp32)
        wT = sb("wT", [P, NB, D], fp32)
        src_rows = sb("src_rows", [NG, GE], i32)
        dst_rows = sb("dst_rows", [NG, GE], i32)
        wgt_rows = sb("wgt_rows", [NG, GE], fp32)
        src_rf = sb("src_rf", [NG, GE], fp32)
        dst_rf = sb("dst_rf", [NG, GE], fp32)
        lohi = sb("lohi", [NG, 2], fp32)
        span = sb("span", [NG, 1], fp32)
        table = sb("table", [NG, 2], fp32)
        slow_f = sb("slow_f", [1, NG], fp32)
        slows_f = sb("slows_f", [1, NG], fp32)

        bk = [bank(f"bank{i}", [P, 512]) for i in range(8)]

        x_in = sem("x_in")
        x_read = sem("x_read")
        b1_taken = sem("b1_taken")
        w_in = sem("w_in")
        pads_set = sem("pads_set")
        edges_in = sem("edges_in")
        consts = sem("consts")
        zero_set = sem("zero_set")
        acc_init = sem("acc_init")
        pool_own = sem("pool_own")
        dve_own = sem("dve_own")
        dve_step = sem("dve_step")
        pool_steps = sem("pool_steps")
        dve_steps = sem("dve_steps")
        act_steps = sem("act_steps")
        pe_steps = sem("pe_steps")
        sp_steps = sem("sp_steps")
        gate_in = sem("gate_in")
        later_in = sem("later_in")
        b1_in = sem("b1_in")
        b1_turned = sem("b1_turned")
        w_t = sem("w_t")
        wT_ready = sem("wT_ready")
        mv_ready = sem("mv_ready")
        std_ready = sem("std_ready")
        shift_ready = sem("shift_ready")
        xn_ready = sem("xn_ready")
        xn_turned = sem("xn_turned")
        xnT_ready = sem("xnT_ready")
        h_done = sem("h_done")
        h_copied = sem("h_copied")
        h_stored = sem("h_stored")
        src_stored = sem("src_stored")
        table_ready = sem("table_ready")
        table_stored = sem("table_stored")
        table_back = sem("table_back")
        floats_ready = sem("floats_ready")
        cols_turned = sem("cols_turned")
        cols_taken = sem("cols_taken")
        src_b_in = [sem(f"src_b_in{q}") for q in range(GB)]
        h_in = [sem(f"h_in{q}") for q in range(GB)]
        gathered = sem("gathered")
        rows_ready = sem("rows_ready")
        dst_ready = sem("dst_ready")
        pick_ready = sem("pick_ready")
        mixed = sem("mixed")
        mix_ready = sem("mix_ready")
        summed = sem("summed")
        msg_ready = sem("msg_ready")
        added = [sem(f"added{c}") for c in range(COPIES)]
        w1_in = [sem(f"w1_in{q}") for q in range(2)]
        w2_in = [sem(f"w2_in{q}") for q in range(2)]

        def turn_loop(engine, body):
            body(0)
            with engine.Fori(1, WT) as t:
                body(t)

        RING = 4
        A = ROWS // P
        ZA = zeros.shape[1] // D

        def load_src(engine, i, q):
            engine.dma_start(src_b[:, q, :], src_dram[ds(i * GB + q, 1), :].to_broadcast([P, GE])).then_inc(src_b_in[q], 16)

        def earlier(j):
            return j - RING + 1 if j >= RING else (j + RING if j + RING < WB else j) - WB + 1

        with nc.Block() as block:
            @block.sync
            def _(sp):
                sp.wait_ge(pads_set, 3)
                for rows, given in ((src_rows, src), (dst_rows, dst), (wgt_rows, edge_weight)):
                    sp.dma_start(rows[0:FULL, :], given[0:FULL * GE].rearrange("(g e) -> g e", e=GE)).then_inc(edges_in, 16)
                    sp.dma_start(rows[FULL:FULL + 1, 0:REST], given[FULL * GE:NE].rearrange("(g e) -> g e", g=1)).then_inc(edges_in, 16)
                sp.dma_start(w_rows[:], gnn_w.rearrange("(b p) d -> p b d", p=P)).then_inc(w_in, 16)
                sp.dma_start(b1_rows[:], b1.rearrange("e (b p) -> (e b) p", p=P)).then_inc(b1_in, 16)
                for t in range(WT - 1):
                    sp.dma_start(x1[:, t * WB:(t + 1) * WB, :],
                                 x[t * WB * P:(t + 1) * WB * P, :].rearrange("(w p) d -> p w d", p=P)).then_inc(x_in, 16)
                sp.wait_ge(pads_set, 4)
                w0 = (WT - 1) * WB
                sp.dma_start(x1[:, w0:NW - 1, :],
                             x[w0 * P:(NW - 1) * P, :].rearrange("(w p) d -> p w d", p=P)).then_inc(x_in, 16)
                sp.dma_start(x1[0:LASTW, NW - 1, :], x[(NW - 1) * P:N, :]).then_inc(x_in, 16)
                sp.dma_start(gate_sb[:], gate_w.rearrange("(b p) e -> p b e", p=P)).then_inc(gate_in, 16)
                sp.dma_start(gate_bb[:], gate_b.partition_broadcast(P)).then_inc(gate_in, 16)
                sp.dma_start(acc[0][0:(NW - 1) * P, :].rearrange("(p a) d -> p (a d)", p=P),
                             x[0:(NW - 1) * P, :].rearrange("(p a) d -> p (a d)", p=P)).then_inc(acc_init, 16)
                sp.dma_start(acc[0][(NW - 1) * P:N, :], x[(NW - 1) * P:N, :]).then_inc(acc_init, 16)
                sp.wait_ge(zero_set, 1)
                sp.dma_start(acc[0][N:NP, :], zeros[0:NP - N, 0:D]).then_inc(acc_init, 16)
                sp.dma_start(acc[0][NP:ROWS, :], zeros[:, 0:D]).then_inc(acc_init, 16)
                for c in range(1, COPIES):
                    rows = acc[c].rearrange("(p a) d -> p (a d)", p=P)
                    for a in range(0, A, ZA):
                        sp.dma_start(rows[:, a * D:(a + ZA) * D], zeros[:]).then_inc(acc_init, 16)

            @block.gpsimd
            def _(pool):
                link = Chain(pool, pool_own)
                pool.memset(src_rows[:], 0).then_inc(pads_set, 1)
                pool.memset(dst_rows[:], N - 1).then_inc(pads_set, 1)
                pool.memset(wgt_rows[:], 0.0).then_inc(pads_set, 1)
                pool.memset(x1[:, NW - 1, :], 0.0).then_inc(pads_set, 1)
                for pads in (x1[:, NW:NWT, :], rstd2[:, NW:NWT], shift2[:, NW:NWT]):
                    pool.memset(pads, 0.0)
                link(pool.memset(ident[:], 0.0))
                pool.affine_select(out=ident[:], in_=ident[:], compare_op=ALU.not_equal, fill=1.0, base=0,
                                   pattern=[[-1, P]], channel_multiplier=1).then_inc(consts, 1)
                link(pool.memset(ones[:], 1.0))
                pool.affine_select(out=before[:], in_=ones[:], compare_op=ALU.is_gt, fill=0.0, base=0,
                                   pattern=[[-1, P]], channel_multiplier=1).then_inc(consts, 1)
                pool.memset(ones_b[:], 1.0).then_inc(consts, 1)
                pool.affine_select(out=upper_f[:], in_=ones[:], compare_op=ALU.is_gt, fill=0.0, base=0,
                                   pattern=[[1, P]], channel_multiplier=-1).then_inc(consts, 1)
                pool.iota(iota_i[:], [[1, P]], base=0, channel_multiplier=0).then_inc(consts, 1)
                pool.iota(part_i[:], [[0, 1]], base=0, channel_multiplier=1).then_inc(consts, 1)
                pool.memset(eps[:], EPS).then_inc(consts, 1)
                pool.memset(zeros[:], 0.0).then_inc(zero_set, 1)

            @block.scalar
            def _(act):
                act.wait_ge(edges_in, 96)
                act.dma_start(src_dram, src_rows[:]).then_inc(src_stored, 16)
                act.wait_ge(table_ready, 1)
                act.dma_start(table_dram, table[:]).then_inc(table_stored, 16)
                act.wait_ge(table_stored, 16)
                act.dma_start(table_b[:], table_dram.partition_broadcast(P)).then_inc(table_back, 16)
                act.wait_ge(src_stored, 16)
                for q in range(GB):
                    load_src(act, 0, q)

                def store_h(t):
                    act.wait_ge(h_copied, t * WB + WB)
                    act.dma_start(h_rows_dram[ds(t * (WB * P), WB * P), :].rearrange("(w p) d -> p w d", p=P),
                                  x1[:, ds(t * WB, WB), :]).then_inc(h_stored, 16)

                def copy_h(t, j):
                    act.wait_ge(h_done, t * WB + (j + 1))
                    act.sem_inc(act_steps, 1)
                    act.activation(x1[:, ds(t * WB + j, 1), :].rearrange("p w d -> p (w d)"), bk[4 + j % RING][:, 0:D],
                                   ACT.Copy).then_inc(h_copied, 1)

                act.wait_ge(mv_ready, 1)
                act.activation(std[:], mv[:, :, 1], ACT.Sqrt, bias=eps[:]).then_inc(std_ready, 1)
                act.wait_ge(shift_ready, 1)

                def body(t):
                    for j in range(WB):
                        await_turn(act, xn_turned, t, WB, j + 1 - WB)
                        act.activation(xn[:, j, :], x1[:, ds(t * WB + j, 1), :].rearrange("p w d -> p (w d)"), ACT.Identity,
                                       bias=shift[:, ds(t * WB + j, 1)], scale=rstd[:, ds(t * WB + j, 1)]).then_inc(xn_ready, 1)
                        if j >= LAG:
                            copy_h(t, j - LAG)
                        elif not isinstance(t, int):
                            copy_h(t - 1, j - LAG + WB)
                            if j == LAG - 1:
                                store_h(t - 1)
                turn_loop(act, body)
                for j in range(WB - LAG, WB):
                    copy_h(WT - 1, j)
                store_h(WT - 1)

            @block.vector
            def _(dve):
                link = Chain(dve, dve_own)
                v = nc.vector
                dve.wait_ge(consts, 7)
                link(v.tensor_copy(iota_f[:], iota_i[:]))
                v.tensor_copy(upper[:], upper_f[:])
                link(v.tensor_copy(part_f[:], part_i[:]))
                link(v.tensor_scalar(junk_row[:], part_f[:], float(JUNK), None, ALU.add))
                dve.wait_ge(edges_in, 96)
                v.tensor_copy(dst_rf[:], dst_rows[:]).then_inc(floats_ready, 1)
                v.tensor_copy(src_rf[:], src_rows[:]).then_inc(floats_ready, 1)
                dve.wait_ge(floats_ready, 1)
                v.tensor_reduce(lohi[:, 0:1], dst_rf[:], AX.X, ALU.min)
                link(v.tensor_reduce(lohi[:, 1:2], dst_rf[:], AX.X, ALU.max))
                link(v.tensor_scalar(table[:, 0:1], lohi[:, 0:1], float(NP - P), None, ALU.min))
                link(v.tensor_tensor(span[:], lohi[:, 1:2], table[:, 0:1], ALU.subtract))
                v.tensor_scalar(table[:, 1:2], span[:], float(P - 1), None, ALU.is_gt).then_inc(table_ready, 1)
                for n, field in enumerate((DST, SRC, WGT)):
                    for half in range(2):
                        dve.wait_ge(cols_turned, 2 * n + half + 1)
                        v.tensor_copy(cols[:, :, field, 4 * half:4 * half + 4],
                                      bk[6 + half][:, 0:4 * NG].rearrange("p (j g) -> p g j", j=4)).then_inc(cols_taken, 1)
                for b in range(NB):
                    dve.wait_ge(w_t, b + 1)
                    v.tensor_copy(wT[:, b, :], bk[b][:, 0:D]).then_inc(wT_ready, 1)
                dve.wait_ge(b1_turned, 1)
                v.tensor_copy(b1_cols[:], bk[2][:, 0:EX * FB]).then_inc(b1_taken, 1)
                dve.wait_ge(x_in, 16 * (WT + 1))
                with dve.Fori(0, WT) as t:
                    for j in range(WB):
                        s = v.bn_stats(stats[:, ds(t * WB + j, 1), :].rearrange("p w s -> p (w s)"),
                                       x1[:, ds(t * WB + j, 1), :].rearrange("p w d -> p (w d)"))
                    s.then_inc(x_read, 1)
                dve.wait_ge(x_read, WT)
                for w in range(NW):
                    s = v.bn_aggr(mv[:, w, :], stats[:, w, :])
                s.then_inc(mv_ready, 1)
                dve.wait_ge(std_ready, 1)
                link(v.reciprocal(rstd[:], std[:]))
                v.scalar_tensor_tensor(shift[:], mv[:, :, 0], -1.0, rstd[:], ALU.mult, ALU.mult).then_inc(shift_ready, 1)

                def body(t):
                    for j in range(WB):
                        dve.wait_ge(xn_turned, t * WB + (j + 1))
                        await_turn(dve, h_done, t, WB, j + 1 - WB)
                        v.tensor_copy(xnT[:, j, :, :], bk[j % RING][:, 0:D].rearrange("p (b n) -> p b n", b=NB)).then_inc(xnT_ready, 1)
                turn_loop(dve, body)
                dve.wait_ge(cols_taken, 6)
                dve.wait_ge(table_back, 16)
                lo = table_b[:, :, 0:1].to_broadcast([P, NG, GT])
                slow = table_b[:, :, 1:2].to_broadcast([P, NG, GT])
                rel, off = cols[:, :, REL, :], cols[:, :, OFF, :]
                v.tensor_scalar(off, cols[:, :, SRC, :], junk_row[:], None, ALU.subtract)
                v.tensor_copy(table_i[:], table_b[0:1, :, :].rearrange("p g c -> p (g c)"))
                link(v.tensor_copy(slow_f[:], table_b[0:1, :, 1:2].rearrange("p g c -> p (g c)")))
                link(v.tensor_tensor_scan(slows_f[:], ones[0:1, 0:NG], slow_f[:], 0.0, ALU.mult, ALU.add))
                v.tensor_scalar(gathers_i[:], slows_f[:], 16.0 * GT, None, ALU.mult)
                link(v.tensor_tensor(rel, cols[:, :, DST, :], lo, ALU.subtract))
                link(v.tensor_scalar(rel, rel, part_f[:], None, ALU.subtract))
                link(v.tensor_scalar(table_b[:, :, 1:2], table_b[:, :, 1:2], -1.0, 1.0, ALU.mult, ALU.add))
                link(v.tensor_tensor(rel, rel, slow, ALU.mult))
                link(v.tensor_scalar(rel, rel, part_f[:], None, ALU.add))

            @block.tensor
            def _(pe):
                pe.wait_ge(consts, 7)
                for n, rows in enumerate((dst_rf, src_rf, wgt_rows)):
                    pe.wait_ge(floats_ready, min(n + 1, 2))
                    for half in range(2):
                        if n > 0:
                            pe.wait_ge(cols_taken, 2 * n + half - 1)
                        for j in range(4):
                            e = (4 * half + j) * P
                            s = nc.tensor.transpose(bk[6 + half][:, j * NG:(j + 1) * NG], rows[:, e:e + P], ident[0:NG, 0:NG])
                        s.then_inc(cols_turned, 1)
                pe.wait_ge(w_in, 16)
                for b in range(NB):
                    for a in range(NB):
                        s = nc.tensor.transpose(bk[b][:, a * P:(a + 1) * P], w_rows[:, a, b * P:(b + 1) * P], ident[:])
                    s.then_inc(w_t, 1)
                pe.wait_ge(b1_in, 16)
                nc.tensor.transpose(bk[2][:, 0:EX * FB], b1_rows[:], ident[0:EX * FB, 0:EX * FB]).then_inc(b1_turned, 1)
                pe.wait_ge(wT_ready, NB)
                pe.wait_ge(b1_taken, 1)
                pe.wait_ge(cols_taken, 6)

                def product(t, j):
                    pe.wait_ge(xnT_ready, t * WB + (j + 1))
                    await_turn(pe, h_copied, t, WB, earlier(j))
                    for b in range(NB):
                        s = nc.tensor.matmul(bk[4 + j % RING][:, 0:D], xnT[:, j, b, :], wT[:, b, :],
                                             start=b == 0, stop=b == NB - 1)
                    s.then_inc(h_done, 1)

                def body(t):
                    for j in range(WB):
                        pe.wait_ge(xn_ready, t * WB + (j + 1))
                        await_turn(pe, xnT_ready, t, WB, earlier(j))
                        for b in range(NB):
                            s = nc.tensor.transpose(bk[j % RING][:, b * P:(b + 1) * P], xn[:, j, b * P:(b + 1) * P],
                                                    ident[:])
                        s.then_inc(xn_turned, 1)
                        if j > 0:
                            product(t, j - 1)
                        elif not isinstance(t, int):
                            product(t - 1, WB - 1)
                turn_loop(pe, body)
                product(WT - 1, WB - 1)
        prepare.close()

        def sb(name, shape, dt):
            return layer1.enter_context(nc.sbuf_tensor(name, shape, dt))

        cols_s = sb("cols_s", [P, GB, 5, GT], fp32)
        h_buf = sb("h_buf", [P, GB, GT, D], fp32)
        dup = sb("dup", [P, GB, GT], fp32)
        row_f = sb("row_f", [P, GB, GT], fp32)
        row_i = sb("row_i", [P, GB, GT], i32)
        dst_i = sb("dst_i", [P, GB, GT], i32)
        merge = sb("merge", [P, GB, GT, P], fp32)
        pick = sb("pick", [P, GB, GT, P], fp32)
        mix = sb("mix", [P, 2, 2, P], fp32)
        msg = sb("msg", [P, 4, 2, D], fp32)

        def turns(engine, body):
            body(0)
            with engine.Fori(1, GTURNS) as i:
                body(i)

        def load_w1(engine, e, q):
            engine.dma_start(w1_sb[:, q, :, :], w1[ds(e, 1), :, :].rearrange("e (b p) f -> p (e b) f", p=P)).then_inc(w1_in[q], 16)

        def load_w2(engine, e, q):
            engine.dma_start(w2_sb[:, q, :, :], w2[ds(e, 1), :, :].rearrange("e (b p) d -> p (e b) d", p=P)).then_inc(w2_in[q], 16)

        with nc.Block() as block:
            @block.sync
            def _(sp):
                def body(i):
                    for q in range(GB):
                        if not isinstance(i, int):
                            await_turn(sp, pick_ready, i, GB * GT, GT * (q + 1) - GB * GT)
                            load_src(sp, i, q)
                        slow = sp.value_load(table_i[0:1, ds(i * (2 * GB) + (2 * q + 1), 1)], min_val=0, max_val=1)
                        lo = sp.value_load(table_i[0:1, ds(i * (2 * GB) + 2 * q, 1)], min_val=0, max_val=NP - P)
                        await_turn(sp, summed, i, PT, PAIRS * (q + 1) - PT)
                        sp.sem_inc(sp_steps, 1)
                        with sp.If(slow == 0):
                            sp.dma_start(h_buf[:, q, 0, :], h_rows_dram[ds(lo, P), :]).then_inc(h_in[q], 16)
                        sp.nop()
                sp.wait_ge(h_stored, 16 * WT)
                turns(sp, body)

            @block.gpsimd
            def _(pool):
                def settled():
                    pool.sem_inc(pool_steps, 1)

                def body(i):
                    for q in range(GB):
                        pool.wait_ge(dst_ready, i * GB + (q + 1))
                        slow = pool.value_load(table_i[0:1, ds(i * (2 * GB) + (2 * q + 1), 1)], min_val=0, max_val=1)
                        with pool.If(slow == 1):
                            await_turn(pool, summed, i, PT, PAIRS * (q + 1) - PT)
                            settled()
                            for j in range(GT):
                                pool.indirect_dma_start(h_buf[:, q, j, :], None, h_rows_dram,
                                                        bass.IndirectOffsetOnAxis(ap=dst_i[:, q, j:j + 1], axis=0)).then_inc(gathered, 16)
                            pool.wait_ge(gathered, pool.value_load(gathers_i[0:1, ds(i * GB + q, 1)], min_val=16 * GT, max_val=16 * GT * NG))
                            pool.sem_inc(h_in[q], 16)
                        pool.wait_ge(rows_ready, i * GB + (q + 1))
                        for j in range(GT):
                            u = q * GT + j
                            c = u % COPIES
                            if j % 2 == 0:
                                pool.wait_ge(msg_ready, i * PT + (u // 2 + 1))
                            per = 16 * GB * GT // COPIES
                            await_turn(pool, added[c], i, per, 16 * (u // COPIES))
                            settled()
                            pool.indirect_dma_start(acc[c], bass.IndirectOffsetOnAxis(ap=row_i[:, q, j:j + 1], axis=0),
                                                    msg[:, (u // 2) % 4, j % 2, :], None,
                                                    compute_op=ALU.add).then_inc(added[c], 16)
                pool.wait_ge(gate_in, 32)
                pool.wait_ge(h_stored, 16 * WT)
                pool.wait_ge(acc_init, 16 * (4 + (COPIES - 1) * A // ZA))
                turns(pool, body)
                for c in range(COPIES):
                    pool.wait_ge(added[c], 16 * NG * GT // COPIES)

            @block.vector
            def _(dve):
                link = Chain(dve, dve_step)
                v = nc.vector

                def body(i):
                    link.enter(i, 3 * GB)
                    for q in range(GB):
                        link(v.tensor_copy(cols_s[:, q, :, :], cols[:, ds(i * GB + q, 1), :, :].rearrange("p g f j -> p (g f) j")))
                        await_turn(dve, summed, i, PT, PAIRS * (q + 1) - PT)
                        v.tensor_copy(dst_i[:, q, :], cols_s[:, q, DST, :]).then_inc(dst_ready, 1)
                        await_turn(dve, mixed, i, PT, PAIRS * (q + 1) - PT)
                        dve.wait_ge(src_b_in[q], i * 16 + 16)
                        for j in range(GT):
                            s = v.scalar_tensor_tensor(merge[:, q, j, :], src_b[:, q, j * P:(j + 1) * P], cols_s[:, q, SRC, j:j + 1], before[:],
                                                       ALU.is_equal, ALU.mult, accum_out=dup[:, q, j:j + 1])
                        link(s)
                        for j in range(GT):
                            v.tensor_scalar(merge[:, q, j, :], src_b[:, q, j * P:(j + 1) * P], cols_s[:, q, SRC, j:j + 1],
                                            cols_s[:, q, WGT, j:j + 1], ALU.is_equal, ALU.mult)
                            v.tensor_scalar(pick[:, q, j, :], iota_f[:], cols_s[:, q, REL, j:j + 1], None,
                                            ALU.is_equal).then_inc(pick_ready, 1)
                        link(v.scalar_tensor_tensor(row_f[:, q, :], dup[:, q, :], 0.0, cols_s[:, q, OFF, :], ALU.is_equal, ALU.mult))
                        for c in range(COPIES):
                            per = 16 * GB * GT // COPIES
                            await_turn(dve, added[c], i, per, 16 * GT // COPIES * (q + 1) - per)
                        v.tensor_scalar(row_i[:, q, :], row_f[:, q, :], junk_row[:], None, ALU.add).then_inc(rows_ready, 1)
                turns(dve, body)

            @block.tensor
            def _(pe):
                def sums(i, k, slow):
                    q = k // PAIRS
                    if k % PAIRS == 0:
                        pe.wait_ge(h_in[q], i * 16 + 16)
                    pe.wait_ge(mix_ready, i * PT + (k + 1))
                    await_turn(pe, msg_ready, i, PT, k + 1 - 4)
                    for e in range(2):
                        j = (2 * k + e) % GT
                        s = nc.tensor.matmul(bk[2 + k % 4][:, e * D:(e + 1) * D], mix[:, k % 2, e, :],
                                             h_buf[:, q, ds(slow * j, 1), :].rearrange("p j d -> p (j d)"), start=True, stop=True)
                    s.then_inc(summed, 1)


                def body(i):
                    prev = i - 1
                    slow = None
                    for k in range(PT):
                        q = k // PAIRS
                        pe.wait_ge(pick_ready, i * (GB * GT) + (2 * k + 2))
                        await_turn(pe, mix_ready, i, PT, k + 1 - 2)
                        for e in range(2):
                            j = (2 * k + e) % GT
                            s = nc.tensor.matmul(bk[k % 2][:, e * P:(e + 1) * P], pick[:, q, j, :], merge[:, q, j, :], start=True, stop=True)
                        s.then_inc(mixed, 1)
                        if k == 0:
                            if isinstance(i, int):
                                pass
                            else:
                                sl = pe.value_load(table_i[0:1, ds(i * (2 * GB) - 1, 1)], min_val=0, max_val=1)
                                sums(prev, PT - 1, sl)
                        else:
                            if (k - 1) % PAIRS == 0:
                                slow = pe.value_load(table_i[0:1, ds(i * (2 * GB) + (2 * ((k - 1) // PAIRS) + 1), 1)], min_val=0, max_val=1)
                            sums(i, k - 1, slow)
                turns(pe, body)
                sl = pe.value_load(table_i[0:1, 2 * NG - 1:2 * NG], min_val=0, max_val=1)
                sums(GTURNS - 1, PT - 1, sl)

            @block.scalar
            def _(act):
                def take_msg(i, k):
                    act.wait_ge(summed, i * PT + (k + 1))
                    for c in ((2 * k) % COPIES, (2 * k + 1) % COPIES):
                        per = 16 * GB * GT // COPIES
                        await_turn(act, added[c], i, per, 16 * ((2 * k - 8) // COPIES + 1))
                    act.activation(msg[:, k % 4, :, :], bk[2 + k % 4][:, 0:2 * D].rearrange("p (e d) -> p e d", e=2),
                                   ACT.Copy).then_inc(msg_ready, 1)

                def body(i):
                    for k in range(PT):
                        act.wait_ge(mixed, i * PT + (k + 1))
                        await_turn(act, summed, i, PT, k + 1 - 2)
                        act.activation(mix[:, k % 2, :, :], bk[k % 2][:, 0:2 * P].rearrange("p (e m) -> p e m", e=2),
                                       ACT.Copy).then_inc(mix_ready, 1)
                        if k > 0:
                            take_msg(i, k - 1)
                        elif not isinstance(i, int):
                            take_msg(i - 1, PT - 1)
                turns(act, body)
                take_msg(GTURNS - 1, PT - 1)

        layer1.close()

        def window_turns(engine, body):
            body(0, 0, 2)
            with engine.Fori(0, (WT - 3) // 2) as i:
                body(i * 2 + 1, 1, 2)
                body(i * 2 + 2, 0, 2)
            body(WT - 2, 1, 1)
            body(WT - 1, 0, 0)

        gate_stage = ctx.enter_context(ExitStack())

        def sb(name, shape, dt):
            return gate_stage.enter_context(nc.sbuf_tensor(name, shape, dt))

        K2 = 2 * WB
        PAIRED = [range(j, min(j + 2, WB)) for j in range(0, WB, 2)]
        NPAIR = len(PAIRED)
        EARLY = 3
        parts = [[sb(f"part{c}_{q}", [P, WB, D], fp32) for c in range(1, COPIES)] for q in range(2)]
        stats2 = sb("stats2", [P, WB, 6], fp32)
        mv2 = sb("mv2", [P, WB, 2], fp32)
        std2 = sb("std2", [P, WB], fp32)
        xg = sb("xg", [P, WB, D], fp32)
        xr = [sb(f"xr{q}", [P, WB, RW], fp32) for q in range(2)]
        xgT = sb("xgT", [P, 2, 2, NB, P], fp32)
        logits = sb("logits", [P, WB, EX], fp32)
        top8 = sb("top8", [P, WB, 8], fp32)
        idx8 = sb("idx8", [P, WB, 8], u32)
        choice = sb("choice", [P, WB, 2], fp32)
        hot_f = sb("hot_f", [P, K2, EX], fp32)
        hot = sb("hot", [P, K2, EX], bf16)
        hot_sum = sb("hot_sum", [P, EX], fp32)
        ranks = sb("ranks", [P, K2, EX], fp32)
        slot_f = sb("slot_f", [P, K2], fp32)
        slot_i = sb("slot_i", [P, 2, K2], i32)
        gap = sb("gap", [P, NW], fp32)
        ratio = sb("ratio", [P, NW], fp32)
        total = sb("total", [P, NW], fp32)

        x1_in = [[sem(f"x1_in{c}_{q}") for c in range(COPIES)] for q in range(2)]
        parts_summed = sem("parts_summed")
        x1_ready = sem("x1_ready")
        mv2_ready = sem("mv2_ready")
        std2_ready = sem("std2_ready")
        norm2_ready = sem("norm2_ready")
        xg_ready = sem("xg_ready")
        xr_ready = sem("xr_ready")
        xg_turned = sem("xg_turned")
        xgT_ready = sem("xgT_ready")
        gated = sem("gated")
        logits_taken = sem("logits_taken")
        hot_ready = sem("hot_ready")
        ranked = sem("ranked")
        slots_ready = sem("slots_ready")
        sent = [sem(f"sent{q}") for q in range(2)]
        gate_own = sem("gate_own")
        counted = sem("counted")
        counts_ready = sem("counts_ready")
        filled = [sem(f"filled{q}") for q in range(2)]
        gap_ready = sem("gap_ready")
        ratio_ready = sem("ratio_ready")

        def fill(engine, q):
            engine.wait_ge(counts_ready, 1)
            with engine.Fori(0, EX // 2) as i:
                e = i * 2 + q
                count = engine.value_load(counts_i[0:1, ds(e, 1)], min_val=0, max_val=NP)
                engine.dma_start(slots_dram[ds(e * CAP + count, P), :], filler[:, q, :]).then_inc(filled[q], 16)

        with nc.Block() as block:
            @block.sync
            def _(sp):
                def body(t, q, more):
                    await_turn(sp, x1_ready, t, 1, -1)
                    for c in (2, 3, 0, 1):
                        to = x1[:, ds(t * WB, WB), :] if c == 0 else parts[q][c - 1][:]
                        sp.dma_start(to, acc[c][ds(t * (WB * P), WB * P), :].rearrange("(w p) d -> p w d", p=P)).then_inc(x1_in[q][c], 16)
                window_turns(sp, body)
                sp.wait_ge(slots_ready, WT - 1)
                for q in range(2):
                    load_w1(sp, q, q)
                    load_w2(sp, q, q)
                for to, given in ((b2_b, b2), (gamma_b, gamma), (beta_b, beta)):
                    sp.dma_start(to[:], given.partition_broadcast(P)).then_inc(later_in, 16)
                fill(sp, 0)
                sp.wait_ge(filled[0], 16 * EX // 2)
                sp.wait_ge(later_in, 16 * 3)

            @block.gpsimd
            def _(pool):
                def body(t, q, more):
                    pool.wait_ge(slots_ready, t + 1)
                    pool.wait_ge(xr_ready, t + 1)
                    pool.sem_inc(pool_steps, 1)
                    for n in range(K2):
                        pool.indirect_dma_start(slots_dram, bass.IndirectOffsetOnAxis(ap=slot_i[:, q, n:n + 1], axis=0),
                                                xr[q][:, n // 2, :], None).then_inc(sent[q], 16)
                window_turns(pool, body)
                pool.wait_ge(sent[0], 16 * K2 * ((WT + 1) // 2))
                pool.wait_ge(sent[1], 16 * K2 * (WT // 2))

            @block.scalar
            def _(act):
                def deviations(t):
                    act.wait_ge(mv2_ready, t + 1)
                    act.activation(std2[:], mv2[:, :, 1], ACT.Sqrt, bias=eps[:]).then_inc(std2_ready, 1)

                def norm(to, t, j):
                    w = t * WB + j
                    return act.activation(to, x1[:, ds(w, 1), :].rearrange("p w d -> p (w d)"), ACT.Identity,
                                          bias=shift2[:, ds(w, 1)], scale=rstd2[:, ds(w, 1)])

                def rows(t, q):
                    await_turn(act, sent[q], t, 8 * K2, -8 * K2 * q)
                    act.sem_inc(act_steps, 1)
                    for j in range(WB):
                        s = norm(xr[q][:, j, 0:D], t, j)
                    s.then_inc(xr_ready, 1)

                def body(t, q, more):
                    act.wait_ge(norm2_ready, t + 1)
                    await_turn(act, xg_turned, t, NPAIR, 0)
                    act.sem_inc(act_steps, 1)
                    for j in range(WB):
                        norm(xg[:, j, :], t, j).then_inc(xg_ready, 1)
                    for g, windows in enumerate(PAIRED):
                        n = len(windows)
                        act.wait_ge(xg_turned, t * NPAIR + (g + 1))
                        await_turn(act, gated, t, NPAIR, g - 1)
                        act.activation(xgT[:, g % 2, 0:n, :, :], bk[g % 2][:, 0:n * D].rearrange("p (w b n) -> p w b n", w=n, b=NB),
                                       ACT.Copy).then_inc(xgT_ready, 1)
                    if more > 0:
                        deviations(t + 1)
                    rows(t, q)
                deviations(0)
                window_turns(act, body)
                act.wait_ge(gap_ready, 1)
                act.activation(ratio[:], gap[:], ACT.Exp).then_inc(ratio_ready, 1)
                fill(act, 1)
                act.wait_ge(filled[1], 16 * EX // 2)

            @block.tensor
            def _(pe):
                def turn_windows(t, g):
                    pe.wait_ge(xg_ready, t * WB + (PAIRED[g][-1] + 1))
                    await_turn(pe, xgT_ready, t, NPAIR, g - 1)
                    for w, j in enumerate(PAIRED[g]):
                        for b in range(NB):
                            s = nc.tensor.transpose(bk[g % 2][:, (w * NB + b) * P:(w * NB + b + 1) * P],
                                                    xg[:, j, b * P:(b + 1) * P], ident[:])
                    s.then_inc(xg_turned, 1)

                def sum_parts(t, q, windows=range(WB)):
                    if windows[0] == 0:
                        for c in range(2, COPIES):
                            pe.wait_ge(x1_in[q][c], t * 8 + (16 - 8 * q))
                        await_turn(pe, x1_ready, t, 1, 0)
                    pe.sem_inc(pe_steps, 1)
                    for j in windows:
                        for c in range(2, COPIES):
                            s = nc.tensor.matmul(bk[4 + j // 2][:, (j % 2) * D:(j % 2 + 1) * D], ident[:], parts[q][c - 1][:, j, :],
                                                 start=c == 2, stop=c == COPIES - 1)
                        s.then_inc(parts_summed, 1)

                def body(t, q, more):
                    await_turn(pe, logits_taken, t, 1, 0)
                    turn_windows(t, 0)
                    for g, windows in enumerate(PAIRED):
                        if g + 1 < NPAIR:
                            turn_windows(t, g + 1)
                        pe.wait_ge(xgT_ready, t * NPAIR + (g + 1))
                        for w, j in enumerate(windows):
                            for b in range(NB):
                                s = nc.tensor.matmul(bk[2][:, j * EX:(j + 1) * EX], xgT[:, g % 2, w, b, :], gate_sb[:, b, :],
                                                     start=b == 0, stop=b == NB - 1)
                        s.then_inc(gated, 1)
                    if more == 2:
                        sum_parts(t + 2, q, range(0, EARLY))
                    pe.wait_ge(hot_ready, t + 1)
                    nc.tensor.matmul(bk[3][:, 0:K2 * EX], upper[:], hot[:].rearrange("p n e -> p (n e)"),
                                     start=True, stop=False, skip_group_check=True)
                    for n in range(1, K2):
                        nc.tensor.matmul(bk[3][:, n * EX:K2 * EX], ones_b[:], hot[:, 0:K2 - n, :].rearrange("p n e -> p (n e)"),
                                         start=False, stop=False, skip_group_check=True)
                    nc.tensor.matmul(bk[3][:, 0:K2 * EX].rearrange("p (n e) -> p n e", e=EX), ones_b[:],
                                     carry[:, None, :].to_broadcast([P, K2, EX]),
                                     start=False, stop=True, skip_group_check=True).then_inc(ranked, 1)
                    if more == 2:
                        sum_parts(t + 2, q, range(EARLY, WB))
                sum_parts(0, 0)
                sum_parts(1, 1)
                window_turns(pe, body)
                pe.wait_ge(counted, 1)
                nc.tensor.matmul(bk[0][0:1, 0:EX], ones_b[:, 0:1], carry[:], start=True, stop=True).then_inc(counted, 1)

            @block.vector
            def _(dve):
                link = Chain(dve, gate_own)
                v = nc.vector

                def sum_and_measure(t, q):
                    for c in range(2):
                        dve.wait_ge(x1_in[q][c], t * 8 + (16 - 8 * q))
                    here = x1[:, ds(t * WB, WB), :]
                    link(v.tensor_tensor(here, here, parts[q][0][:], ALU.add))
                    for j in range(0, WB, 2):
                        n = min(2, WB - j)
                        dve.wait_ge(parts_summed, t * WB + (j + n))
                        here = x1[:, ds(t * WB + j, n), :]
                        s = v.tensor_tensor(here, here, bk[4 + j // 2][:, 0:n * D].rearrange("p (w d) -> p w d", d=D), ALU.add)
                    link(s)
                    dve.sem_inc(x1_ready, 1)
                    for j in range(WB):
                        s = v.bn_stats(stats2[:, j, :], x1[:, ds(t * WB + j, 1), :].rearrange("p w d -> p (w d)"))
                    link(s)
                    dve.sem_inc(dve_steps, 1)
                    for j in range(WB):
                        s = v.bn_aggr(mv2[:, j, :], stats2[:, j, :])
                    s.then_inc(mv2_ready, 1)

                def norm_factors(t):
                    dve.wait_ge(std2_ready, t + 1)
                    rs, sh = rstd2[:, ds(t * WB, WB)], shift2[:, ds(t * WB, WB)]
                    link(v.reciprocal(rs, std2[:]))
                    link(v.scalar_tensor_tensor(sh, mv2[:, :, 0], -1.0, rs, ALU.mult, ALU.mult))
                    dve.sem_inc(norm2_ready, 1)

                def body(t, q, more):
                    if more == 2:
                        link.enter(t, 16)
                    elif more == 1:
                        link.leave(WT - 2)
                    if more > 0:
                        norm_factors(t + 1)
                    dve.wait_ge(gated, t * NPAIR + NPAIR)
                    s = v.tensor_tensor(logits[:], bk[2][:, 0:WB * EX].rearrange("p (w e) -> p w e", e=EX),
                                        gate_bb[:, None, :].to_broadcast([P, WB, EX]), ALU.add)
                    link(s)
                    dve.sem_inc(logits_taken, 1)
                    for j in range(WB):
                        s = v.max(top8[:, j, :], logits[:, j, :])
                    link(s)
                    dve.sem_inc(dve_steps, 1)
                    for j in range(WB):
                        s = v.max_index(idx8[:, j, :], top8[:, j, :], logits[:, j, :])
                    link(s)
                    v.tensor_copy(top2[:, ds(t * WB, WB), :], top8[:, :, 0:2])
                    link(v.tensor_copy(choice[:], idx8[:, :, 0:2]))
                    for k in range(2):
                        s = v.tensor_tensor(hot_f[:].rearrange("p (w k) e -> p w k e", k=2)[:, :, k, :],
                                            iota_f[:, None, 0:EX].to_broadcast([P, WB, EX]),
                                            choice[:, :, k:k + 1].to_broadcast([P, WB, EX]), ALU.is_equal)
                    link(s)
                    v.tensor_reduce(hot_sum[:], hot_f[:].rearrange("p n e -> p e n"), AX.X, ALU.add)
                    link(v.tensor_copy(hot[:], hot_f[:]))
                    dve.sem_inc(hot_ready, 1)
                    dve.wait_ge(ranked, t + 1)
                    link(v.tensor_tensor(ranks[:], bk[3][:, 0:K2 * EX].rearrange("p (n e) -> p n e", e=EX),
                                         expert_base[:, None, :].to_broadcast([P, K2, EX]), ALU.add))
                    link(v.tensor_tensor(ranks[:], ranks[:], hot_f[:], ALU.mult))
                    v.tensor_tensor(carry_f[:], carry_f[:], hot_sum[:], ALU.add)
                    link(v.tensor_reduce(slot_f[:], ranks[:], AX.X, ALU.add))
                    v.tensor_copy(carry[:], carry_f[:])
                    await_turn(dve, sent[q], t, 8 * K2, -8 * K2 * q)
                    v.tensor_copy(xr[q][:, :, TOKEN], tok[:])
                    v.tensor_copy(xr[q][:, :, CHOICE], choice[:, :, 0])
                    link(v.tensor_copy(slot_i[:, q, :], slot_f[:]))
                    link(v.tensor_scalar(tok[:], tok[:], float(WB * P), None, ALU.add))
                    dve.sem_inc(slots_ready, 1)
                    if more == 2:
                        sum_and_measure(t + 2, q)
                for q in range(2):
                    v.memset(xr[q][:, :, D:RW], 0.0)
                v.memset(carry_f[:], 0.0)
                v.memset(carry[:], 0.0)
                link(v.memset(filler[:], 0.0))
                for j in range(WB):
                    v.tensor_scalar(tok[:, j:j + 1], part_f[:], float(j * P), None, ALU.add)
                v.tensor_scalar(expert_base[:], iota_f[:, 0:EX], float(CAP), None, ALU.mult)
                for q in range(2):
                    v.tensor_scalar(filler[:, q, TOKEN:TOKEN + 1], part_f[:], float(NP + q * P), None, ALU.add)
                link(v.memset(filler[:, :, CHOICE:CHOICE + 1], -1.0))
                sum_and_measure(0, 0)
                norm_factors(0)
                sum_and_measure(1, 1)
                window_turns(dve, body)
                dve.sem_inc(counted, 1)
                dve.wait_ge(counted, 2)
                link(v.tensor_copy(counts_f[:], bk[0][0:1, 0:EX]))
                v.tensor_copy(counts_i[:], counts_f[:]).then_inc(counts_ready, 1)
                link(v.tensor_scalar(ntiles_i[:], counts_f[:], float(P - 1), None, ALU.add))
                link(v.tensor_scalar(ntiles_i[:], ntiles_i[:], P.bit_length() - 1, None, ALU.arith_shift_right))
                link(v.tensor_scalar(ntiles_f[:], ntiles_i[:], 1.0, None, ALU.max))
                link(v.tensor_tensor_scan(ends_f[:], ones[0:1, 0:EX], ntiles_f[:], 0.0, ALU.mult, ALU.add))
                v.memset(tiles_i[:, 0:1], 0)
                link(v.tensor_copy(tiles_i[:, 1:EX + 1], ends_f[:]))
                v.tensor_tensor(gap[:], top2[:, :, 1], top2[:, :, 0], ALU.subtract).then_inc(gap_ready, 1)
                dve.wait_ge(ratio_ready, 1)
                link(v.tensor_scalar(total[:], ratio[:], 1.0, None, ALU.add))
                link(v.reciprocal(first_w[:], total[:]))
                link(v.tensor_tensor(second_w[:], ratio[:], first_w[:], ALU.mult))
        gate_stage.close()

        xn2 = ctx.enter_context(nc.sbuf_tensor("xn2", [P, NWT, D], fp32))
        expert_stage = ctx.enter_context(ExitStack())

        def sb(name, shape, dt):
            return expert_stage.enter_context(nc.sbuf_tensor(name, shape, dt))

        xt = sb("xt", [P, RW], fp32)
        xtT = sb("xtT", [P, NB, P], fp32)
        held = sb("held", [P, 2], fp32)
        other = sb("other", [P, 1], fp32)
        to_i = sb("to_i", [P, 2, 1], i32)
        start_i = sb("start_i", [P, 3], i32)
        hT = sb("hT", [P, FB, P], fp32)
        y_sb = sb("y_sb", [P, 2, D], fp32)

        xt_in = sem("xt_in")
        xt_turned = sem("xt_turned")
        xt_read = sem("xt_read")
        xtT_ready = sem("xtT_ready")
        up_done = sem("up_done")
        hT_ready = sem("hT_ready")
        down_done = sem("down_done")
        y_ready = sem("y_ready")
        y_sent = [sem(f"y_sent{q}") for q in range(2)]
        xn2_ready = sem("xn2_ready")
        first_set = sem("first_set")
        expert_own = sem("expert_own")

        def experts(engine, start, tile, end):
            with engine.Fori(0, EX // 2) as i:
                for q in range(2):
                    e = i * 2 + q
                    lo = engine.value_load(tiles_i[0:1, ds(e, 1)], min_val=0, max_val=MAXT)
                    hi = engine.value_load(tiles_i[0:1, ds(e + 1, 1)], min_val=1, max_val=MAXT)
                    start(i, e, q)
                    with engine.Fori(lo, hi) as s:
                        tile(i, e, q, s, lo)
                    end(i, e, q, hi)

        assert -(-2 * N // P) >= 2 * NW

        def half_of(windows, s):
            return windows[:].rearrange("p w (h d) -> p (w h) d", h=2)[:, ds(s, 1), :].rearrange("p s d -> p (s d)")

        def nothing(*_):
            pass

        with nc.Block() as block:
            @block.sync
            def _(sp):
                def tile(i, e, q, s, lo):
                    sp.wait_ge(xt_turned, s + 1)
                    sp.wait_ge(xt_read, s + 1)
                    sp.dma_start(xt[:], slots_dram[ds((e * CAP + (s - lo) * P).with_bounds(min_val=0, max_val=EX * CAP - P), P), :]).then_inc(xt_in, 16)

                experts(sp, nothing, tile, nothing)
                tiles = sp.value_load(tiles_i[0:1, EX:EX + 1], min_val=EX, max_val=MAXT)
                sp.wait_ge(xt_turned, tiles + 1)
                sp.wait_ge(xt_read, tiles + 1)
                sp.dma_start(xt[:], slots_dram[0:P, :]).then_inc(xt_in, 16)
                sp.wait_ge(xt_in, tiles * 16 + 16)
                sp.sem_inc(sp_steps, 1)

            @block.gpsimd
            def _(pool):
                pool.wait_ge(first_set, 1)
                for n in range(3):
                    if n == 2:
                        pool.wait_ge(y_sent[1], 16)
                    pool.indirect_dma_start(y_dram, bass.IndirectOffsetOnAxis(ap=start_i[:, n:n + 1], axis=0),
                                            y_sb[:, min(n, 1), :], None).then_inc(y_sent[min(n, 1)], 16)

                def tile(i, e, q, s, lo):
                    pool.wait_ge(y_ready, s + 2)
                    pool.sem_inc(pool_steps, 1)
                    with pool.If((s & 1) == 0):
                        pool.indirect_dma_start(y_dram, bass.IndirectOffsetOnAxis(ap=to_i[:, 0, :], axis=0),
                                                y_sb[:, 0, :], None).then_inc(y_sent[0], 16)
                    with pool.Else():
                        pool.indirect_dma_start(y_dram, bass.IndirectOffsetOnAxis(ap=to_i[:, 1, :], axis=0),
                                                y_sb[:, 1, :], None).then_inc(y_sent[1], 16)
                    pool.nop()
                experts(pool, nothing, tile, nothing)
                tiles = pool.value_load(tiles_i[0:1, EX:EX + 1], min_val=EX, max_val=MAXT)
                pool.wait_ge(y_sent[0], ((tiles + 1) >> 1) * 16 + 16)
                pool.wait_ge(y_sent[1], (tiles >> 1) * 16 + 32)

            @block.scalar
            def _(act):
                act.sem_inc(hT_ready, 1)

                def tile(i, e, q, s, lo):
                    act.wait_ge(down_done, s + 1)
                    for f in range(FB):
                        act.wait_ge(up_done, s * FB + (f + 1))
                        act.activation(hT[:, f, :], bk[f][:, 0:P], ACT.Relu,
                                       bias=b1_cols[:, ds(e * FB + f, 1)]).then_inc(hT_ready, 1)

                    act.activation(half_of(xn2, s), half_of(x1, s), ACT.Identity,
                                   bias=shift2[:, ds(s >> 1, 1)], scale=rstd2[:, ds(s >> 1, 1)]).then_inc(xn2_ready, 1)

                def end(i, e, q, hi):
                    with act.If(i < EX // 2 - 1):
                        act.wait_ge(up_done, hi * FB)
                        act.sem_inc(act_steps, 1)
                        load_w1(act, (e + 2).with_bounds(min_val=2, max_val=EX - 1), q)
                        act.wait_ge(down_done, hi + 1)
                        act.sem_inc(act_steps, 1)
                        load_w2(act, (e + 2).with_bounds(min_val=2, max_val=EX - 1), q)
                    act.nop()
                experts(act, nothing, tile, end)

            @block.tensor
            def _(pe):
                def turn_tile():
                    for b in range(NB):
                        s = nc.tensor.transpose(bk[4][:, b * P:(b + 1) * P], xt[:, b * P:(b + 1) * P], ident[:])
                    s.then_inc(xt_turned, 1)

                pe.sem_inc(down_done, 1)
                pe.sem_inc(xt_turned, 1)
                pe.wait_ge(xt_in, 16)
                turn_tile()

                def start(i, e, q):
                    pe.wait_ge(w1_in[q], i * 16 + 16)
                    pe.sem_inc(pe_steps, 1)

                def tile(i, e, q, s, lo):
                    pe.wait_ge(xtT_ready, s + 1)
                    pe.wait_ge(hT_ready, s * FB + 1)
                    for f in range(FB):
                        for b in range(NB):
                            m = nc.tensor.matmul(bk[f][:, 0:P], w1_sb[:, q, b, f * P:(f + 1) * P], xtT[:, b, :],
                                                 start=b == 0, stop=b == NB - 1)
                        m.then_inc(up_done, 1)
                    pe.wait_ge(xt_in, s * 16 + 32)
                    turn_tile()
                    pe.wait_ge(y_ready, s + 1)
                    pe.wait_ge(w2_in[q], i * 16 + 16)
                    for f in range(FB):
                        pe.wait_ge(hT_ready, s * FB + (f + 2))
                        m = nc.tensor.matmul(bk[5][:, 0:D], hT[:, f, :], w2_sb[:, q, f, :], start=f == 0, stop=f == FB - 1)
                    m.then_inc(down_done, 1)
                experts(pe, start, tile, nothing)

            @block.vector
            def _(dve):
                link = Chain(dve, expert_own)
                v = nc.vector

                def take_tile():
                    v.tensor_copy(held[:], xt[:, TOKEN:CHOICE + 1]).then_inc(xt_read, 1)
                    v.tensor_copy(xtT[:], bk[4][:, 0:D].rearrange("p (b n) -> p b n", b=NB)).then_inc(xtT_ready, 1)

                dve.sem_inc(xt_read, 1)
                dve.sem_inc(y_ready, 1)
                link(v.memset(y_sb[:], 0.0))
                for n in range(3):
                    s = v.tensor_scalar(start_i[:, n:n + 1], part_f[:], float(2 * NP + (2 + n) * P), None, ALU.add)
                s.then_inc(first_set, 1)
                dve.wait_ge(xt_turned, 2)
                take_tile()

                def tile(i, e, q, s, lo):
                    dve.wait_ge(xt_read, s + 2)
                    v.tensor_scalar(other[:], held[:, 1:2], iota_f[:, ds(e, 1)], float(NP), ALU.not_equal, ALU.mult).then_inc(expert_own, 1)
                    dve.wait_ge(expert_own, s * 2 + 2)
                    dve.wait_ge(y_sent[0], (s >> 1) * 16 + 16)
                    dve.wait_ge(y_sent[1], ((s + 1) >> 1) * 16 + 16)
                    v.tensor_tensor(to_i[:, ds(s & 1, 1), :].rearrange("p a b -> p (a b)"), other[:], held[:, 0:1], ALU.add).then_inc(expert_own, 1)
                    dve.wait_ge(expert_own, s * 2 + 3)
                    dve.wait_ge(xt_turned, s + 3)
                    dve.wait_ge(up_done, s * FB + FB)
                    take_tile()
                    dve.wait_ge(down_done, s + 2)
                    v.tensor_tensor(y_sb[:, ds(s & 1, 1), :].rearrange("p a d -> p (a d)"), bk[5][:, 0:D], b2_b[:, ds(e, 1), :].rearrange("p e d -> p (e d)"), ALU.add).then_inc(y_ready, 1)
                    dve.wait_ge(xn2_ready, s + 1)
                    v.tensor_tensor(half_of(x1, s), half_of(x1, s), beta_b[:, ds((s & 1) * (D // 2), D // 2)], ALU.add)
                experts(dve, nothing, tile, nothing)
        expert_stage.close()

        last_stage = ctx.enter_context(ExitStack())

        def sb(name, shape, dt):
            return last_stage.enter_context(nc.sbuf_tensor(name, shape, dt))

        ya = [sb(f"ya{q}", [P, WB, D], fp32) for q in range(2)]
        yb = [sb(f"yb{q}", [P, WB, D], fp32) for q in range(2)]
        o = [sb(f"o{q}", [P, WB, D], fp32) for q in range(2)]
        stats3 = sb("stats3", [P, WB, 6], fp32)
        mv3 = sb("mv3", [P, WB, 2], fp32)
        std3 = sb("std3", [P, WB], fp32)
        rs3 = sb("rs3", [P, WB], fp32)
        sh3 = sb("sh3", [P, WB], fp32)

        HALVES = [(0, WB // 2 + 1), (WB // 2 + 1, WB // 2)]
        LATE = 2
        ya_in = [sem(f"ya_in{q}") for q in range(2)]
        yb_in = [sem(f"yb_in{q}") for q in range(2)]
        y_summed = sem("y_summed")
        mv3_ready = sem("mv3_ready")
        std3_ready = sem("std3_ready")
        norm3_ready = sem("norm3_ready")
        yn_ready = sem("yn_ready")
        last_ready = sem("last_ready")
        scaled = sem("scaled")
        out_ready = sem("out_ready")
        out_sent = [sem(f"out_sent{q}") for q in range(2)]
        last_own = sem("last_own")

        with nc.Block() as block:
            @block.sync
            def _(sp):
                def load(t, q):
                    for k, (to, there) in enumerate(((ya[q], ya_in[q]), (yb[q], yb_in[q]))):
                        sp.dma_start(to[:], y_dram[ds(t * (WB * P) + k * NP, WB * P), :].rearrange("(w p) d -> p w d", p=P)).then_inc(there, 16)

                def body(t, q, more):
                    if more == 2:
                        sp.wait_ge(y_summed, t + 1)
                        load(t + 2, q)
                    if more > 0:
                        for k, (w, n) in enumerate(HALVES):
                            sp.wait_ge(out_ready, t * 2 + (k + 1))
                            sp.dma_start(out[ds(t * (WB * P) + w * P, n * P), :].rearrange("(w p) d -> p w d", p=P),
                                         o[q][:, w:w + n, :]).then_inc(out_sent[q], 16)
                load(0, 0)
                load(1, 1)
                window_turns(sp, body)
                w0 = (WT - 1) * WB
                sp.wait_ge(out_ready, 2 * WT - 1)
                sp.dma_start(out[w0 * P:(w0 + LATE) * P, :].rearrange("(w p) d -> p w d", p=P), o[0][:, 0:LATE, :]).then_inc(out_sent[0], 16)
                sp.wait_ge(last_ready, 1)
                sp.dma_start(out[(w0 + LATE) * P:(NW - 1) * P, :].rearrange("(w p) d -> p w d", p=P), o[0][:, LATE:WB - 1, :]).then_inc(out_sent[0], 16)
                sp.dma_start(out[(NW - 1) * P:N, :], o[0][0:LASTW, WB - 1, :]).then_inc(out_sent[0], 16)
                sp.wait_ge(out_sent[0], 32 * ((WT - 1) // 2) + 48)
                sp.wait_ge(out_sent[1], 32 * (WT // 2))

            @block.scalar
            def _(act):
                def body(t, q, more):
                    act.wait_ge(mv3_ready, t + 1)
                    act.activation(std3[:], mv3[:, :, 1], ACT.Sqrt, bias=eps[:]).then_inc(std3_ready, 1)
                    act.wait_ge(norm3_ready, t + 1)
                    for j in range(WB):
                        s = act.activation(o[q][:, j, :], o[q][:, j, :], ACT.Identity, bias=sh3[:, j:j + 1], scale=rs3[:, j:j + 1])
                        if j + 1 in (HALVES[1][0], WB):
                            s.then_inc(yn_ready, 1)
                window_turns(act, body)

            @block.gpsimd
            def _(pool):
                def body(t, q, more):
                    for k, (w, n) in enumerate(HALVES if more else [(0, LATE)]):
                        here = o[q][:, w:w + n, :]
                        pool.wait_ge(yn_ready, t * 2 + (k + 1))
                        pool.tensor_tensor(here, here, gamma_b[:, None, :].to_broadcast([P, n, D]), ALU.mult).then_inc(scaled, 1)
                        pool.wait_ge(scaled, t * 2 + (k + 1))
                        pool.sem_inc(pool_steps, 1)
                        pool.tensor_tensor(here, here, x1[:, ds(t * WB + w, n), :], ALU.add).then_inc(out_ready, 1)
                window_turns(pool, body)

            @block.vector
            def _(dve):
                link = Chain(dve, last_own)
                v = nc.vector

                def add_first(t, q):
                    dve.wait_ge(ya_in[q], t * 8 + (16 - 8 * q))
                    dve.sem_inc(dve_steps, 1)
                    for j in range(WB):
                        s = v.scalar_tensor_tensor(ya[q][:, j, :], ya[q][:, j, :], first_w[:, ds(t * WB + j, 1)],
                                                   xn2[:, ds(t * WB + j, 1), :].rearrange("p w d -> p (w d)"), ALU.mult, ALU.add)
                    link(s)

                def body(t, q, more):
                    if more == 2:
                        link.enter(t, 5)
                    elif more == 1:
                        link.leave(WT - 2)
                    dve.wait_ge(yb_in[q], t * 8 + (16 - 8 * q))
                    await_turn(dve, out_sent[q], t, 16, -16 * q)
                    dve.sem_inc(dve_steps, 1)
                    for j in range(WB):
                        s = v.scalar_tensor_tensor(o[q][:, j, :], yb[q][:, j, :], second_w[:, ds(t * WB + j, 1)], ya[q][:, j, :], ALU.mult, ALU.add)
                    link(s)
                    dve.sem_inc(y_summed, 1)
                    for j in range(WB):
                        s = v.bn_stats(stats3[:, j, :], o[q][:, j, :])
                    link(s)
                    dve.sem_inc(dve_steps, 1)
                    for j in range(WB):
                        s = v.bn_aggr(mv3[:, j, :], stats3[:, j, :])
                    s.then_inc(mv3_ready, 1)
                    dve.wait_ge(std3_ready, t + 1)
                    await_turn(dve, yn_ready, t, 2, 0)
                    link(v.reciprocal(rs3[:], std3[:]))
                    link(v.scalar_tensor_tensor(sh3[:], mv3[:, :, 0], -1.0, rs3[:], ALU.mult, ALU.mult))
                    dve.sem_inc(norm3_ready, 1)
                    if more > 0:
                        add_first(t + 1, 1 - q)
                add_first(0, 0)
                window_turns(dve, body)
                late = o[0][:, LATE:WB, :]
                dve.wait_ge(yn_ready, 2 * WT)
                link(v.tensor_tensor(late, late, gamma_b[:, None, :].to_broadcast([P, WB - LATE, D]), ALU.mult))
                link(v.tensor_tensor(late, late, x1[:, NW - WB + LATE:NW, :], ALU.add))
                dve.sem_inc(last_ready, 1)
        last_stage.close()


_INS = ['x', 'src', 'dst', 'edge_weight', 'L0_gnn_W', 'L0_ffn_gate_w', 'L0_ffn_gate_b', 'L0_ffn_w1', 'L0_ffn_b1',
        'L0_ffn_w2', 'L0_ffn_b2', 'L0_ffn_gamma', 'L0_ffn_beta']
_OUTS = [((6250, 256), 'float32')]


def kernel(**inputs):
    import numpy as _np
    import concourse.bacc as _bacc
    from concourse import mybir as _mybir
    from concourse.bass_utils import run_bass_kernel_spmd as _run

    nc = _bacc.Bacc("TRN2", target_bir_lowering=False, num_devices=1)
    arrays, args = {}, []
    for name in _INS:
        a = _np.ascontiguousarray(inputs[name])
        arrays[f"in_{name}_dram"] = a
        args.append(nc.dram_tensor(f"in_{name}_dram", a.shape, _mybir.dt.from_np(a.dtype), kind="ExternalInput").ap())
    for i, (shape, dtype) in enumerate(_OUTS):
        dt = _mybir.dt.from_np(_np.dtype(dtype))
        args.append(nc.dram_tensor(f"out_{i}_dram", shape, dt, kind="ExternalOutput").ap())
    gnn_moe_kernel(nc, *args)
    r = _run(nc, [arrays], core_ids=[0])
    got = tuple(r.results[0][f"out_{i}_dram"] for i in range(len(_OUTS)))
    return got[0]
```
